# Optimizing a Trainium2 kernel written in Bass

```python
import numpy as np
import jax
import jax.numpy as jnp

def _softmax(x, axis=-1):
    return jax.nn.softmax(x, axis=axis)

def _gelu(x):
    return jax.nn.gelu(x, approximate=True)

def _silu(x):
    return jax.nn.silu(x)

def _sigmoid(x):
    return jax.nn.sigmoid(x)

def _layernorm(x, axis=-1, eps=1e-05):
    m = jnp.mean(x, axis=axis, keepdims=True)
    v = jnp.var(x, axis=axis, keepdims=True)
    return (x - m) / jnp.sqrt(v + eps)

def _scatter_add(tgt, idx, src, axis=0):
    return tgt.at[idx].add(src)

def _segment_sum(src, seg, n):
    return jax.ops.segment_sum(src, seg, n)
kernel_name = 'mk_flamingo_gated_d1_seqx_r4_c8bf11'

def setup_inputs(seed: int=0):
    np.random.seed(seed)
    _w = jnp.asarray

    def _rec_inputs():
        import jax
        import jax.numpy as jnp
        _rk = jax.random.key(seed)
        x = -0.000125 + 0.9999 * jax.random.normal(jax.random.fold_in(_rk, 1), (4, 512, 512), jnp.float32)
        _lenS = 512 - jax.random.randint(jax.random.fold_in(_rk, 7), (4,), 0, max(1, 512 // 4) + 1, jnp.int32)
        _lenS2 = 512 - jax.random.randint(jax.random.fold_in(_rk, 8), (4,), 0, max(1, 512 // 4) + 1, jnp.int32)
        itok_BxS_13_99985 = jax.random.randint(jax.random.fold_in(_rk, 11), (4, 512), 13, 99986, jnp.int32)
        _ctx_2048P = jax.random.normal(jax.random.fold_in(_rk, 12), (4, 16, 512), jnp.float32)
        _ctx_2048c = jax.random.dirichlet(jax.random.fold_in(_rk, 512), 0.3 * jnp.ones((16,), jnp.float32), (4, 512))
        _ctx_2048t = jnp.einsum('bsk,bkd->bsd', _ctx_2048c, _ctx_2048P)
        _ctx_2048t = _ctx_2048t * jax.lax.rsqrt(jnp.mean(jnp.square(_ctx_2048t)) + 1e-12) * 0.953939
        ctx_2048 = 6.82029e-06 + 0.0200006 * (_ctx_2048t + 0.3 * jax.random.normal(jax.random.fold_in(_rk, 612), (4, 512, 512), jnp.float32))
        _g = jax.random.normal(jax.random.fold_in(_rk, 9001), (2, 1), jnp.float32)
        _g = jnp.sign(_g) * jnp.maximum(jnp.abs(_g), 1.0) + (_g == 0) * 1.0
        g_xattn = _g[0]
        g_ffn = _g[1]
        return (x, itok_BxS_13_99985, ctx_2048, g_xattn, g_ffn)
    x, itok_BxS_13_99985, ctx_2048, g_xattn, g_ffn = _rec_inputs()

    def _L0_xattn_setup():
        import jax, jax.numpy as jnp
        import numpy as np
        B, S, D = (4, 1024, 512)
        E = 4
        F = 2048 // E
        VOCAB = 25000
        key = jax.random.key(seed)
        k1, k2, k3, k4, k5 = jax.random.split(key, 5)
        hidden_states = jax.random.normal(k1, (B, S, D), dtype=jnp.float32)
        token_ids = jax.random.randint(k2, (B, S), 0, VOCAB, dtype=jnp.int64)
        Wg = jax.random.normal(k3, (E, F, D), dtype=jnp.float32) * 0.02
        Wu = jax.random.normal(k4, (E, F, D), dtype=jnp.float32) * 0.02
        Wd = jax.random.normal(k5, (E, D, F), dtype=jnp.float32) * 0.02
        return {'hidden_states': hidden_states, 'token_ids': token_ids, 'Wg': Wg, 'Wu': Wu, 'Wd': Wd}
    _L0_xattn_all = _L0_xattn_setup()
    _L0_xattn_in = {k: v for k, v in _L0_xattn_all.items() if k in ()}
    del _L0_xattn_all

    def _L0_ffn_setup():
        import jax, jax.numpy as jnp
        import numpy as np
        B_, S, D = (2, 512, 512)
        F_ = 2048
        R = 16
        H = 16
        HD = D // H
        MOD_SCALE = 0.1
        EPS = 1e-06

        def _rmsnorm(x, w):
            v = jnp.mean(x * x, axis=-1, keepdims=True)
            return x * jax.lax.rsqrt(v + EPS) * w

        def _attention(x, Wq, Wk, Wv, Wo):
            b, s, d = x.shape
            q = (x @ Wq.T).reshape(b, s, H, HD)
            k = (x @ Wk.T).reshape(b, s, H, HD)
            v = (x @ Wv.T).reshape(b, s, H, HD)
            scores = jnp.einsum('bqhd,bkhd->bhqk', q, k) / np.sqrt(HD).astype(np.float32)
            causal = jnp.tril(jnp.ones((s, s), bool))
            scores = jnp.where(causal, scores, jnp.finfo(scores.dtype).min)
            probs = jax.nn.softmax(scores, axis=-1)
            out = jnp.einsum('bhqk,bkhd->bqhd', probs, v).reshape(b, s, d)
            return out @ Wo.T
        key = jax.random.key(seed)
        ks = jax.random.split(key, 12)
        sd = 0.02
        return {'hidden_states': jax.random.normal(ks[0], (B_, S, D), jnp.float32), 'ln1_w': jnp.ones((D,), jnp.float32), 'ln2_w': jnp.ones((D,), jnp.float32), 'Wq': jax.random.normal(ks[1], (D, D), jnp.float32) * sd, 'Wk': jax.random.normal(ks[2], (D, D), jnp.float32) * sd, 'Wv': jax.random.normal(ks[3], (D, D), jnp.float32) * sd, 'Wo': jax.random.normal(ks[4], (D, D), jnp.float32) * sd, 'A': jax.random.normal(ks[5], (D, R), jnp.float32) * (0.01 / np.sqrt(D)), 'B': jax.random.normal(ks[6], (R, F_), jnp.float32) * (0.01 / np.sqrt(R)), 'W_in_base': jax.random.normal(ks[7], (F_, D), jnp.float32) * sd, 'W_up_base': jax.random.normal(ks[8], (F_, D), jnp.float32) * sd, 'W_down': jax.random.normal(ks[9], (D, F_), jnp.float32) * sd}
    _L0_ffn_all = _L0_ffn_setup()
    _L0_ffn_in = {k: v for k, v in _L0_ffn_all.items() if k in ('ln1_w', 'ln2_w', 'Wq', 'Wk', 'Wv', 'Wo', 'A', 'B', 'W_in_base', 'W_up_base', 'W_down')}
    del _L0_ffn_all
    return {'x': x, 'itok_BxS_13_99985': itok_BxS_13_99985, 'ctx_2048': ctx_2048, 'g_xattn': g_xattn, 'g_ffn': g_ffn, 'L0_ffn_ln1_w': _L0_ffn_in['ln1_w'], 'L0_ffn_ln2_w': _L0_ffn_in['ln2_w'], 'L0_ffn_Wq': _L0_ffn_in['Wq'], 'L0_ffn_Wk': _L0_ffn_in['Wk'], 'L0_ffn_Wv': _L0_ffn_in['Wv'], 'L0_ffn_Wo': _L0_ffn_in['Wo'], 'L0_ffn_A': _L0_ffn_in['A'], 'L0_ffn_B': _L0_ffn_in['B'], 'L0_ffn_W_in_base': _L0_ffn_in['W_in_base'], 'L0_ffn_W_up_base': _L0_ffn_in['W_up_base'], 'L0_ffn_W_down': _L0_ffn_in['W_down']}

def reference(x, itok_BxS_13_99985, ctx_2048, g_xattn, g_ffn, L0_ffn_ln1_w, L0_ffn_ln2_w, L0_ffn_Wq, L0_ffn_Wk, L0_ffn_Wv, L0_ffn_Wo, L0_ffn_A, L0_ffn_B, L0_ffn_W_in_base, L0_ffn_W_up_base, L0_ffn_W_down):
    import jax
    import jax.numpy as jnp

    def _L0_xattn_ref(hidden_states, token_ids, Wg, Wu, Wd):
        import jax, jax.numpy as jnp
        import numpy as np
        B, S, D = (4, 1024, 512)
        E = 4
        F = 2048 // E
        VOCAB = 25000
        tokens_per_expert = VOCAB // E
        tid = jnp.clip(token_ids, 0, VOCAB - 1)
        expert_ids = jnp.minimum(tid // tokens_per_expert, E - 1)
        out = jnp.zeros_like(hidden_states)
        for e in range(E):
            g = jax.nn.silu(jnp.einsum('bsd,fd->bsf', hidden_states, Wg[e]))
            u = jnp.einsum('bsd,fd->bsf', hidden_states, Wu[e])
            y = jnp.einsum('bsf,df->bsd', g * u, Wd[e])
            out = jnp.where((expert_ids == e)[..., None], y, out)
        return out

    def _L0_ffn_ref(hidden_states, ln1_w, ln2_w, Wq, Wk, Wv, Wo, A, B, W_in_base, W_up_base, W_down):
        import jax, jax.numpy as jnp
        import numpy as np
        B_, S, D = (2, 512, 512)
        F_ = 2048
        R = 16
        H = 16
        HD = D // H
        MOD_SCALE = 0.1
        EPS = 1e-06

        def _rmsnorm(x, w):
            v = jnp.mean(x * x, axis=-1, keepdims=True)
            return x * jax.lax.rsqrt(v + EPS) * w

        def _attention(x, Wq, Wk, Wv, Wo):
            b, s, d = x.shape
            q = (x @ Wq.T).reshape(b, s, H, HD)
            k = (x @ Wk.T).reshape(b, s, H, HD)
            v = (x @ Wv.T).reshape(b, s, H, HD)
            scores = jnp.einsum('bqhd,bkhd->bhqk', q, k) / np.sqrt(HD).astype(np.float32)
            causal = jnp.tril(jnp.ones((s, s), bool))
            scores = jnp.where(causal, scores, jnp.finfo(scores.dtype).min)
            probs = jax.nn.softmax(scores, axis=-1)
            out = jnp.einsum('bhqk,bkhd->bqhd', probs, v).reshape(b, s, d)
            return out @ Wo.T
        residual = hidden_states
        x = _rmsnorm(hidden_states, ln1_w)
        attn = _attention(x, Wq, Wk, Wv, Wo)
        mod = MOD_SCALE * jnp.tanh(attn @ A)
        h = _rmsnorm(residual, ln2_w)
        gate_pre = h @ W_in_base.T + mod * (h @ A) @ B
        gate = jax.nn.silu(gate_pre)
        up = h @ W_up_base.T
        mlp_out = gate * up @ W_down.T
        return residual + mlp_out
    x = x + jnp.tanh(g_xattn[0]) * _L0_xattn_ref(_layernorm(x, axis=-1), itok_BxS_13_99985, ctx_2048, ctx_2048, ctx_2048)
    x = x + jnp.tanh(g_ffn[0]) * _L0_ffn_ref(_layernorm(x, axis=-1), L0_ffn_ln1_w, L0_ffn_ln2_w, L0_ffn_Wq, L0_ffn_Wk, L0_ffn_Wv, L0_ffn_Wo, L0_ffn_A, L0_ffn_B, L0_ffn_W_in_base, L0_ffn_W_up_base, L0_ffn_W_down)
    return x

_drawn_inputs = setup_inputs


def setup_inputs(seed=0):
    import zlib

    import numpy as np

    out = dict(_drawn_inputs(seed))
    spreads = {'L0_ffn_ln1_w': (1.0, 0.6), 'L0_ffn_ln2_w': (1.0, 0.2)}
    factors = {'L0_ffn_Wq': 64.0,
     'L0_ffn_Wk': 64.0,
     'L0_ffn_Wv': 64.0,
     'L0_ffn_Wo': 64.0,
     'L0_ffn_A': 64.0,
     'L0_ffn_B': 64.0}
    for name, (base, spread) in spreads.items():
        noise = np.random.default_rng([zlib.crc32(name.encode()), seed]).standard_normal(out[name].shape)
        drawn = base * np.exp(spread * noise) if base else spread * noise
        out[name] = jnp.asarray(drawn.astype(out[name].dtype))
    for name, factor in factors.items():
        out[name] = (out[name] * factor).astype(out[name].dtype)
    return out
```

```python
from contextlib import ExitStack

import concourse.bass as bass
from concourse import mybir

F32 = mybir.dt.float32
F32R = mybir.dt.float32r
I32 = mybir.dt.int32
ALU = mybir.AluOpType
ACT = mybir.ActivationFunctionType
AXX = mybir.AxisListType.X

P = 128
NB, S, D = 4, 512, 512
T = NB * S
DT = D // P
TT = S // P
NT = T // P
E = 4
PER_EXPERT = 25000 // E
ITEMS = T // P + E - 1
EW = DT * D
H, HD, R = 16, 32, 16
QH = P // HD
NQ = H // QH
F = 2048
NCH = F // P
CW = 2 * DT * P
LN_EPS, RMS_EPS = 1e-5, 1e-6
MASKED = -1e30
SCALE = float(HD) ** -0.5
MOD_SCALE = 0.1
HI, LO = 0, 1
Q_LO, Q_HI, K_HI, K_LO = range(4)
GATE, UP, Y0, QKB, ATT = 0, 1, 2, 3, 7
SCORE = {3: (0, 0, 0), 2: (1, 0, 512), 0: (1, 384, 896), 1: (2, 0, 1024)}
TURNED = {0: (4, 0, 0), 1: (5, 0, 512), 3: (5, 384, 896), 2: (6, 0, 1024)}
PACKED = 1280
PARTS = ((HI, HI), (LO, HI), (HI, LO))


def build(nc, x, ids, wexp, wov, amat, bmat, ln, gates, wqk, wmlp, out):
    ctx = ExitStack()
    with ctx:
        def sb(name, shape, dt=F32):
            return ctx.enter_context(nc.sbuf_tensor(name, shape, dt))

        def sem(name):
            return ctx.enter_context(nc.semaphore(name))

        xs = nc.dram_tensor("x_sorted", [T + P, D], F32).ap()
        ys = nc.dram_tensor("y_sorted", [T + P, D], F32).ap()

        big = sb("big", [P, NT, D])
        xt = big[:, 0:4, :]
        hb = big[:, 4:8, :]
        flat = big[:, :, :].rearrange("p a b -> p (a b)")
        prob = [flat[:, 4096 + PACKED * k:4096 + PACKED * (k + 1)] for k in range(2)]
        vp = flat[:, 6656:6656 + TT * H * R].rearrange("p (t h r) -> p t h r", t=TT, h=H)
        stream = sb("stream", [P, 2, EW])
        wstage = sb("wstage", [P, 2, EW])
        wr = sb("wr", [P, 2, E * EW], F32R)
        wrf = wr[:, :, :].rearrange("p a b -> p (a b)")

        def carve(start, n):
            return wrf[:, start:start + n]

        hT = carve(0, 4096).rearrange("p (a d t) -> p a d t", a=2, d=DT)
        wqs = carve(4096, 2048).rearrange("p (a m d c) -> p a m d c", a=2, m=2, d=DT)
        qk = carve(6144, 2048).rearrange("p (m t) -> p m t", m=4)
        pts = carve(8192, 4 * PACKED).rearrange("p (h a c) -> p h a c", h=2, a=2)
        VS = QH * 64 + 64
        vst = carve(8192 + 4 * PACKED, TT * VS).rearrange("p (t c) -> p t c", t=TT)
        vst_v = vst[:, :, 0:QH * 64].rearrange("p t (h c) -> p t h c", h=QH)
        wqk_v = wstage[:, :, :].rearrange("p m (d c) -> p m d c", d=DT)
        braw = flat[0:96, 4096:4096 + F]
        stack = sb("stack", [3 * HD, 2, 2, S], F32R)
        vw = sb("vw", [P, 2, DT, H * R], F32R)
        apad = sb("apad", [P, DT, P], F32R)
        zst = sb("zst", [96, S], F32R)
        bst = sb("bst", [96, F], F32R)
        identr = sb("identr", [P, P], F32R)
        maskr = sb("maskr", [P, P], F32R)
        zeror = sb("zeror", [P, P], F32R)
        wch = sb("wch", [P, 2, 2, CW + D], F32R)
        actr = sb("actr", [P, 2, 2, S], F32R)
        xTs, aTs = actr[:, 0], actr[:, 1]
        ident = sb("ident", [P, P])
        tri = sb("tri", [P, P])
        ones = sb("ones", [P, P])
        xi = sb("xi", [P, D])
        sil = sb("sil", [P, S])
        act_sb = sb("act_sb", [P, S])
        ysb = sb("ysb", [P, D])
        araw = sb("araw", [P, DT, R])
        lns = sb("lns", [P, 2, DT])
        gt = sb("gt", [P, 2])
        tg = sb("tg", [P, 2])
        bd = sb("bd", [P, DT, QH, R])
        idst = sb("idst", [P, NT], I32)
        idf = sb("idf", [P, NT])
        ge = sb("ge", [P, E + 1, NT])
        oh = sb("oh", [P, E, NT])
        cnt = sb("cnt", [P, 2, E * NT])
        cum = sb("cum", [P, E * NT])
        exc = sb("exc", [P, E * NT])
        pe_ = sb("pe_", [P, E, NT])
        posf = sb("posf", [P, NT])
        pos = sb("pos", [P, NT], I32)
        small = sb("small", [P, 16, E])
        lna = sb("lna", [P, 4, 4])
        lnb = sb("lnb", [P, 4, 4])
        bchunk = sb("bchunk", [96, 2, P], F32R)
        asc = sb("asc", [P, DT, R])
        nti = sb("nti", [P, E], I32)
        itf = sb("itf", [P, 20])
        its = sb("its", [P, 3, 20])
        itab = sb("itab", [P, 2, 20], I32)
        st = sb("st", [P, 4, 6])
        mv = sb("mv", [P, 4, 2])
        nr = sb("nr", [P, 12, 4])
        nri = sb("nri", [P, 2, 4], I32)
        nb = sb("nb", [P, 4])
        rs = sb("rs", [P, 2, 4])
        rr = sb("rr", [P, 4])
        haT, att_low, att_sum, zrow = xi[0:R, :], ysb[0:R, :], act_sb[0:R, :], sil[0:R, :]

        bank = [ctx.enter_context(nc.psum_tensor(f"bank{k}", [P, 512], F32)) for k in range(8)]

        ids_in, small_in, wov_in, wqk_in = sem("ids_in"), sem("small_in"), sem("wov_in"), sem("wqk_in")
        b_in = sem("b_in")
        x_in = [sem(f"x_in{g}") for g in range(4)]
        exp_in = [sem(f"exp_in{k}") for k in range(2)]
        exp_hi, exp_lo = sem("exp_hi"), sem("exp_lo")
        const_ok, zero_ok, tail_ok = sem("const_ok"), sem("zero_ok"), sem("tail_ok")
        pool_own, dve_own, act_own = sem("pool_own"), sem("dve_own"), sem("act_own")
        onehot_ok, ranks_ok, pos_ok, items_ok = sem("onehot_ok"), sem("ranks_ok"), sem("pos_ok"), sem("items_ok")
        norm_ok, xn_ok, scattered = sem("norm_ok"), sem("xn_ok"), sem("scattered")
        woa_ok, bd_ok, vw_mm, vw_hi, prep_ok = sem("woa_ok"), sem("bd_ok"), sem("vw_mm"), sem("vw_hi"), sem("prep_ok")
        tanh_ok, wqk_ok = sem("tanh_ok"), sem("wqk_ok")
        a_hi, b_hi = sem("a_hi"), sem("b_hi")
        xi_in, x_turned, xt_hi, xt_lo = sem("xi_in"), sem("x_turned"), sem("xt_hi"), sem("xt_lo")
        h_done, h_silu, h_gated = sem("h_done"), sem("h_silu"), sem("h_gated")
        a_turned, at_hi, at_lo = sem("a_turned"), sem("at_hi"), sem("at_lo")
        y_done, y_copied, y_stored = sem("y_done"), sem("y_copied"), sem("y_stored")
        xt_in, y_in = sem("xt_in"), sem("y_in")
        ln_ok, hb_ok, fin_ok = sem("ln_ok"), sem("hb_ok"), sem("fin_ok")
        hb_turned, ht_hi, ht_lo = sem("hb_turned"), sem("ht_hi"), sem("ht_lo")
        vp_done, vp_copied = sem("vp_done"), sem("vp_copied")
        ha_done, ha_low, ha_ok = sem("ha_done"), sem("ha_low"), sem("ha_ok")
        wq_hi, wq_lo = sem("wq_hi"), sem("wq_lo")
        qk_done, qk_hi, qk_lo = sem("qk_done"), sem("qk_hi"), sem("qk_lo")
        stk = [sem(f"stk{k}") for k in range(2)]
        vst_hi, vst_lo = sem("vst_hi"), sem("vst_lo")
        s_done, nb_ok, exp_ok, pn_ok = sem("s_done"), sem("nb_ok"), sem("exp_ok"), sem("pn_ok")
        p_turned, pt_hi, pt_lo, pv_done = sem("p_turned"), sem("pt_hi"), sem("pt_lo"), sem("pv_done")
        at_low, at_sum, mod_ok, z_ok, zs_hi, zs_ok = (sem(n) for n in ("at_low", "at_sum", "mod_ok", "z_ok", "zs_hi", "zs_ok"))
        cg_in = [sem(f"cg_in{k}") for k in range(2)]
        cd_in = [sem(f"cd_in{k}") for k in range(2)]
        cg_hi, cg_lo, cd_hi, cd_lo = (sem(n) for n in ("cg_hi", "cg_lo", "cd_hi", "cd_lo"))
        apad_ok, bst_ok, vst_zero, rr_ok, ln_own = (sem(n) for n in ("apad_ok", "bst_ok", "vst_zero", "rr_ok", "ln_own"))
        g_done, u_done, g_silu, gu_ok, gu_hi, gu_lo = (sem(n) for n in ("g_done", "u_done", "g_silu", "gu_ok", "gu_hi", "gu_lo"))
        d_done, fin_out, out_in = sem("d_done"), sem("fin_out"), sem("out_in")

        def gu_view(cols):
            return cols.rearrange("p (m d f) -> p m d f", m=2, d=DT)

        def loads_of(b, c):
            half = c // 2
            return b * (16 * NCH // 2) + half * 16 + 16

        x_tiles = x.rearrange("(g j p) d -> g p j d", p=P, j=4)
        out_tiles = out.rearrange("(g j p) d -> g p j d", p=P, j=4)

        block = ctx.enter_context(nc.Block())

        @block.sync
        def _(sp):
            sp.dma_start(idst[:, :], ids).then_inc(ids_in, 16)
            for g in range(4):
                sp.dma_start(big[:, 4 * g:4 * g + 4, :], x_tiles[g]).then_inc(x_in[g], 16)
            for e in range(2):
                sp.dma_start(stream[:, e, :], wexp[:, e, :]).then_inc(exp_in[e], 16)
            sp.dma_start(lns[:, :, :], ln).then_inc(small_in, 16)
            sp.dma_start(gt[:, :], gates.broadcast_to([P, 2])).then_inc(small_in, 16)
            sp.dma_start(araw[:, :, :], amat).then_inc(small_in, 16)
            sp.dma_start(wstage[:, :, :], wov).then_inc(wov_in, 16)
            for e in range(2, E):
                sp.wait_ge(exp_hi, e - 1)
                sp.wait_ge(exp_lo, e - 1)
                sp.dma_start(stream[:, e % 2, :], wexp[:, e, :]).then_inc(exp_in[e % 2], 16)
            sp.wait_ge(zero_ok, 1)
            sp.dma_start(xs[T:T + P, :], ysb[:, :]).then_inc(tail_ok, 16)
            sp.wait_ge(tail_ok, 16)
            sp.wait_ge(vw_mm, 2)
            sp.dma_start(wstage[:, :, :], wqk).then_inc(wqk_in, 16)

            sp.wait_ge(scattered, 16 * NT)
            sp.wait_ge(bst_ok, 1)
            for k in range(3):
                sp.dma_start(braw[32 * k:32 * k + R, :], bmat).then_inc(b_in, 16)

            def item_rows(i):
                sp.wait_ge(items_ok, 1)
                return sp.value_load(itab[0:1, 0, bass.ds(i, 1)], min_val=0, max_val=T)

            def load_item(i):
                sp.dma_start(xi[:, :], xs[bass.ds(item_rows(i), P), :]).then_inc(xi_in, 16)

            def store_item(i):
                rows = item_rows(i)
                sp.wait_ge(y_copied, i + 1)
                sp.dma_start(ys[bass.ds(rows, P), :], ysb[:, :]).then_inc(y_stored, 16)

            sp.wait_ge(items_ok, 1)
            sp.wait_ge(scattered, 16 * NT)
            load_item(0)
            for i in range(1, 3):
                sp.wait_ge(x_turned, i)
                load_item(i)
            with sp.Fori(3, ITEMS) as i:
                sp.wait_ge(x_turned, i)
                load_item(i)
                store_item(i - 3)
            for i in range(ITEMS - 3, ITEMS):
                store_item(i)

            def load_chunk(b, c, par, first=False):
                if not first:
                    sp.wait_ge(cg_lo, b * NCH + c - 1)
                sp.dma_start(stream[:, par, 0:CW], wmlp[:, bass.ds(c, 1), 0:CW]).then_inc(cg_in[par], 16)
                if not first:
                    sp.wait_ge(cd_lo, b * NCH + c - 1)
                sp.dma_start(stream[:, par, CW:CW + D], wmlp[:, bass.ds(c, 1), CW:CW + D]).then_inc(cd_in[par], 16)

            def load_stack(b, q, j):
                g = b * NQ + q
                if j == 0:
                    sp.wait_ge(qk_lo, g * 2 + 2)
                elif type(q) is int and j == 1:
                    pass
                else:
                    sp.wait_ge(s_done, g * (3 * QH) + (j - 1) * 3)
                rows = slice(HD * j, HD * j + HD)
                for k, (a, c) in enumerate(((Q_HI, K_HI), (Q_LO, K_HI), (Q_HI, K_LO))):
                    sp.dma_start(stack[HD * k:HD * k + HD, j % 2, :, :].bitcast(F32),
                                 qk[rows, a:c + 1:c - a, :].bitcast(F32)).then_inc(stk[j % 2], 16)

            def load_x(b):
                sp.dma_start(xt, x_tiles[bass.ds(b, 1)]).then_inc(xt_in, 16)

            def batch(b, last=False):
                for c in range(2):
                    load_chunk(b, c, c, first=True)
                for j in range(QH):
                    load_stack(b, 0, j)
                with sp.Fori(1, NQ) as q:
                    for j in range(QH):
                        load_stack(b, q, j)
                with sp.Fori(1, NCH // 2) as c2:
                    for par in range(2):
                        load_chunk(b, c2 * 2 + par, par)
                sp.wait_ge(fin_out, b + 1)
                sp.dma_start(out_tiles[bass.ds(b, 1)], xt).then_inc(out_in, 16)
                if not last:
                    sp.wait_ge(out_in, b * 16 + 16)
                    load_x(b + 1)

            sp.wait_ge(exp_lo, E)
            load_x(0)
            with sp.Fori(0, NB - 1) as b:
                batch(b)
            batch(NB - 1, last=True)
            sp.wait_ge(out_in, NB * 16)
            sp.wait_ge(y_stored, ITEMS * 16)

        @block.gpsimd
        def _(pool):
            g = nc.gpsimd
            g.memset(ysb[:, :], 0.0).then_inc(zero_ok, 1)
            g.memset(ident[:, :], 0.0).then_inc(pool_own, 1)
            g.memset(ones[:, :], 1.0).then_inc(pool_own, 1)
            g.memset(act_sb[:, :], 0.0).then_inc(pool_own, 1)
            g.memset(zeror[:, :].bitcast(F32), 0.0).then_inc(pool_own, 1)
            g.memset(apad[:, :, :].bitcast(F32), 0.0).then_inc(pool_own, 1)
            g.iota(itab[:, 0, :], [[1, 20]], base=0, channel_multiplier=0).then_inc(pool_own, 1)
            pool.wait_ge(pool_own, 6)
            g.affine_select(out=ident[:, :], in_=ident[:, :], compare_op=ALU.not_equal, fill=1.0,
                            base=0, pattern=[[-1, P]], channel_multiplier=1).then_inc(const_ok, 1)
            g.affine_select(out=tri[:, :], in_=ones[:, :], compare_op=ALU.is_gt, fill=0.0,
                            base=0, pattern=[[1, P]], channel_multiplier=-1).then_inc(const_ok, 1)
            g.affine_select(out=act_sb[:, 0:P], in_=act_sb[:, 0:P], compare_op=ALU.is_ge, fill=MASKED,
                            base=0, pattern=[[-1, P]], channel_multiplier=1).then_inc(const_ok, 1)
            g.tensor_copy(itf[:, :], itab[:, 0, :]).then_inc(const_ok, 1)
            pool.wait_ge(const_ok, 4)
            g.tensor_copy(identr[:, :], ident[:, :]).then_inc(const_ok, 1)
            g.tensor_copy(maskr[:, :], act_sb[:, 0:P]).then_inc(const_ok, 1)
            pool.wait_ge(pos_ok, 1)
            for t in range(NT):
                pool.wait_ge(xn_ok, t + 1)
                g.indirect_dma_start(xs[0:T, :], bass.IndirectOffsetOnAxis(ap=pos[:, t:t + 1], axis=0),
                                     big[:, t, :], None).then_inc(scattered, 16)
            pool.wait_ge(scattered, 16 * NT)
            g.memset(braw, 0.0).then_inc(bst_ok, 1)
            pool.wait_ge(small_in, 48)
            for dt in range(DT):
                ins = g.tensor_scalar(asc[:, dt, :], araw[:, dt, :], lns[:, 1, dt:dt + 1], None, ALU.mult)
            ins.then_inc(pool_own, 1)
            pool.wait_ge(pool_own, 7)
            g.tensor_copy(apad[:, :, 0:R], asc[:, :, :]).then_inc(pool_own, 1)
            pool.wait_ge(pool_own, 8)
            g.tensor_tensor(apad[:, :, 32:32 + R], asc[:, :, :], apad[:, :, 0:R].bitcast(F32),
                            ALU.subtract).then_inc(apad_ok, 1)
            pool.wait_ge(b_in, 48)
            g.tensor_copy(bst[:, :], braw).then_inc(pool_own, 1)
            pool.wait_ge(pool_own, 9)
            g.tensor_tensor(bst[64:96, :], braw[64:96, :], bst[64:96, :].bitcast(F32),
                            ALU.subtract).then_inc(bst_ok, 1)

            pool.wait_ge(bst_ok, 2)
            pool.wait_ge(y_stored, 16 * ITEMS)
            for t in range(NT):
                if t and t % TT == 0:
                    pool.wait_ge(hb_turned, t)
                g.indirect_dma_start(hb[:, t % TT, :], None, ys[0:T, :],
                                     bass.IndirectOffsetOnAxis(ap=pos[:, t:t + 1], axis=0)).then_inc(y_in, 16)

        @block.tensor
        def _(pe):
            def split_product(dst, lhs, rhs, tiles, start=True, stop=True, skip=False):
                n = len(PARTS) * tiles
                i = 0
                for k in range(tiles):
                    for pl, pr in PARTS:
                        mm = pe.matmul(dst, lhs(pl, k), rhs(pr, k), start=start and i == 0,
                                       stop=stop and i == n - 1, skip_group_check=skip)
                        i += 1
                return mm

            pe.wait_ge(const_ok, 6)
            pe.wait_ge(onehot_ok, 1)
            ohf = oh[:, :, :].rearrange("p e t -> p (e t)")
            pe.matmul(bank[0][:, 0:64], tri[:, :], ohf, start=True, stop=True)
            pe.matmul(bank[0][:, 64:128], ones[:, :], ohf, start=True, stop=True).then_inc(ranks_ok, 1)

            pe.wait_ge(wov_in, 16)
            pe.wait_ge(small_in, 48)
            for ct in range(DT):
                for dt in range(DT):
                    mm = pe.matmul(bank[1][:, ct * R:ct * R + R],
                                   wstage[:, 0, dt * D + ct * P:dt * D + ct * P + P], araw[:, dt, :],
                                   start=dt == 0, stop=dt == DT - 1)
            mm.then_inc(woa_ok, 1)
            pe.wait_ge(bd_ok, 1)
            for dt in range(DT):
                for ct in range(DT):
                    mm = pe.matmul(bank[2 + dt // 2][:, 256 * (dt % 2) + 64 * ct:256 * (dt % 2) + 64 * ct + 64],
                                   wstage[:, 1, ct * D + dt * P:ct * D + dt * P + P],
                                   bd[:, ct, :, :].rearrange("p h r -> p (h r)"), start=True, stop=True)
                if dt % 2:
                    mm.then_inc(vw_mm, 1)

            XB, HB, AB, YB = 4, 5, 6, 7
            wflat = wr

            def turn_x(i, first=False):
                pe.wait_ge(xi_in, i * 16 + 16)
                if not first:
                    pe.wait_ge(xt_lo, i)
                for k in range(DT):
                    mm = pe.transpose(bank[XB][:, k * P:k * P + P], xi[:, k * P:k * P + P], ident[:, :])
                mm.then_inc(x_turned, 1)

            def first_product(w, i, first=False):
                pe.wait_ge(xt_lo, i + 1)
                if not first:
                    pe.wait_ge(h_gated, i)
                split_product(bank[HB][:, :], lambda p, k: xTs[:, p, k * P:k * P + P],
                              lambda p, k: wflat[:, p, bass.ds(w + k * D, D)], DT).then_inc(h_done, 1)

            def turn_act(i, first=False):
                pe.wait_ge(h_gated, i + 1)
                if not first:
                    pe.wait_ge(at_lo, i)
                for k in range(DT):
                    mm = pe.transpose(bank[AB][:, k * P:k * P + P], act_sb[:, k * P:k * P + P], ident[:, :])
                mm.then_inc(a_turned, 1)

            def second_product(w, i, first=False):
                pe.wait_ge(at_lo, i + 1)
                if not first:
                    pe.wait_ge(y_copied, i)
                split_product(bank[YB][:, :], lambda p, k: aTs[:, p, k * P:k * P + P],
                              lambda p, k: wflat[:, p, bass.ds(w + k * D, D)], DT).then_inc(y_done, 1)

            def weight_of(i):
                return pe.value_load(itab[0:1, 1, bass.ds(i, 1)], min_val=0, max_val=(E - 1) * EW)

            pe.wait_ge(items_ok, 1)
            pe.wait_ge(exp_hi, E)
            pe.wait_ge(exp_lo, E)
            turn_x(0, first=True)
            first_product(weight_of(0), 0, first=True)
            turn_x(1)
            turn_act(0, first=True)
            first_product(weight_of(1), 1)
            turn_x(2)
            second_product(weight_of(0), 0, first=True)
            turn_act(1)
            with pe.Fori(2, ITEMS - 1) as i:
                first_product(weight_of(i), i)
                turn_x(i + 1)
                second_product(weight_of(i - 1), i - 1)
                turn_act(i)
            last = ITEMS - 1
            first_product(weight_of(last), last)
            second_product(weight_of(last - 1), last - 1)
            turn_act(last)
            second_product(weight_of(last), last)

            pe.wait_ge(prep_ok, 1)
            pe.wait_ge(apad_ok, 1)

            def project(b, q, which):
                n = b * NQ + q
                pe.wait_ge(wq_hi, n + 1)
                pe.wait_ge(wq_lo, n + 1)
                if which:
                    pe.wait_ge(qk_lo, n * 2 + 1)
                split_product(bank[QKB][:, :], lambda p, k: wqs[:, p, which, k, :],
                              lambda p, k: hT[:, p, k, :], DT).then_inc(qk_done, 1)

            def scores(n, par, loads, first=False):
                pe.wait_ge(stk[par], loads)
                if not first:
                    pe.wait_ge(exp_ok, n * 4)
                for i, qt in enumerate((3, 2, 0, 1)):
                    bk, col, _ = SCORE[qt]
                    w = P * (qt + 1)
                    pe.matmul(bank[bk][:, col:col + w], stack[:, par, 0, qt * P:qt * P + P],
                              stack[:, par, 1, 0:w], start=True, stop=False, skip_group_check=True)
                    mm = pe.matmul(bank[bk][:, col + w - P:col + w], identr[:, :], maskr[:, :],
                                   start=False, stop=True, skip_group_check=True)
                    if qt != 2:
                        mm.then_inc(s_done, 1)

            def turn_probs(n, par, first=False):
                pe.wait_ge(pn_ok, n * 4 + 4)
                for kt in (0, 1, 3, 2):
                    bk, col, _ = TURNED[kt]
                    if not first and kt != 3:
                        pe.wait_ge(pt_lo, (n - 1) * 3 + (1, 2, 3)[kt])
                    for qt in range(kt, TT):
                        src = SCORE[qt][2] + kt * P
                        mm = pe.transpose(bank[bk][:, col + (qt - kt) * P:col + (qt - kt) * P + P],
                                          prob[par][:, src:src + P], ident[:, :])
                    if kt != 1:
                        mm.then_inc(p_turned, 1)

            def attend(b, q, n, j):
                pe.wait_ge(pt_lo, n * 3 + 3)
                pe.wait_ge(vst_lo, b * NQ + q + 1)
                for kt in range(TT):
                    _, _, at = TURNED[kt]
                    w = S - kt * P
                    for part in (HI, LO):
                        mm = pe.matmul(bank[ATT][:, kt * P:S], vst[:, kt, 64 * j:64 * j + P],
                                       pts[:, j % 2, part, at:at + w], start=False, stop=False, skip_group_check=True)
                mm.then_inc(pv_done, 1)

            def head_step(b, q, j, ahead):
                n = (b * NQ + q) * QH + j
                if ahead or j < QH - 2:
                    m = b * (H // 2) + q * 2 + (j + 2) // 2
                    scores(n + 2, j % 2, m * 48 + 48)
                if j == 0 and ahead:
                    project(b, q + 1, 1)
                if j == 3 and ahead == 2:
                    project(b, q + 2, 0)
                if ahead or j < QH - 1:
                    turn_probs(n + 1, (j + 1) % 2)
                attend(b, q, n, j)

            def gate_up(b, c, par, first=False):
                n = b * NCH + c
                pe.wait_ge(cg_hi, n + 1)
                pe.wait_ge(cg_lo, n + 1)
                if not first:
                    pe.wait_ge(gu_ok, n)
                split_product(bank[GATE][:, :], lambda p, k: wch[:, par, p, k * P:k * P + P],
                              lambda p, k: hT[:, p, k, :], DT, stop=False)
                pe.matmul(bank[GATE][:, :], bchunk[:, par, :], zst[:, :], start=False,
                          stop=True).then_inc(g_done, 1)
                split_product(bank[UP][:, :], lambda p, k: wch[:, par, p, (DT + k) * P:(DT + k) * P + P],
                              lambda p, k: hT[:, p, k, :], DT).then_inc(u_done, 1)

            def down(b, c, par):
                n = b * NCH + c
                pe.wait_ge(gu_lo, n + 1)
                pe.wait_ge(cd_lo, n + 1)
                for tt in range(TT):
                    mm = split_product(bank[Y0 + tt][:, :], lambda p, k: actr[:, par, p, tt * P:tt * P + P],
                                       lambda p, k: wch[:, par, p, CW:CW + D], 1, start=False, stop=False, skip=True)
                mm.then_inc(d_done, 1)

            with pe.Fori(0, NB) as b:
                pe.wait_ge(hb_ok, b * 4 + 4)
                for dt in range(DT):
                    for tt in range(TT):
                        mm = pe.transpose(bank[dt][:, tt * P:tt * P + P], hb[:, tt, dt * P:dt * P + P], ident[:, :])
                    mm.then_inc(hb_turned, 1)
                pe.wait_ge(ht_lo, b * 4 + 4)
                for tt in range(TT):
                    mm = split_product(bank[4 + tt // 2][:, 256 * (tt % 2):256 * (tt % 2) + 256],
                                       lambda p, k: hT[:, p, k, tt * P:tt * P + P],
                                       lambda p, k: vw[:, p, k, :], DT)
                    if tt % 2:
                        mm.then_inc(vp_done, 1)
                for k in range(DT):
                    for part in (HI, LO):
                        mm = pe.matmul(bank[6][:, :], apad[:, k, :], hT[:, part, k, :],
                                       start=k == 0 and part == HI, stop=k == DT - 1 and part == LO)
                mm.then_inc(ha_done, 1)
                for which in range(2):
                    project(b, 0, which)
                pe.matmul(bank[ATT][:, :], zeror[:, :], hT[:, HI, 0, :], start=True, stop=False,
                          skip_group_check=True).then_inc(pv_done, 1)
                pe.wait_ge(vp_copied, b * 2 + 2)
                pe.wait_ge(ha_ok, b + 1)
                scores(b * H, 0, b * (H // 2) * 48 + 48, first=True)
                scores(b * H + 1, 1, b * (H // 2) * 48 + 48)
                project(b, 1, 0)
                turn_probs(b * H, 0, first=True)
                with pe.Fori(0, NQ - 2) as q:
                    for j in range(QH):
                        head_step(b, q, j, 2)
                for q, ahead in ((NQ - 2, 1), (NQ - 1, 0)):
                    for j in range(QH):
                        head_step(b, q, j, ahead)
                pe.wait_ge(exp_ok, (b + 1) * H * 4)
                pe.wait_ge(zs_ok, b + 1)
                for tt in range(TT):
                    pe.matmul(bank[Y0 + tt][:, :], zeror[:, :], hT[:, HI, 0, :], start=True, stop=False,
                              skip_group_check=True)
                gate_up(b, 0, 0, first=True)
                with pe.Fori(0, NCH // 2 - 1) as c2:
                    gate_up(b, c2 * 2 + 1, 1)
                    down(b, c2 * 2, 0)
                    gate_up(b, c2 * 2 + 2, 0)
                    down(b, c2 * 2 + 1, 1)
                gate_up(b, NCH - 1, 1)
                down(b, NCH - 2, 0)
                down(b, NCH - 1, 1)
                pe.wait_ge(fin_out, b + 1)

        @block.scalar
        def _(act):
            a = nc.scalar

            def copy(dst, src):
                return a.activation(dst, src, ACT.Copy)

            act.wait_ge(small_in, 48)
            a.activation(tg[:, :], gt[:, :], ACT.Tanh).then_inc(tanh_ok, 1)
            for t in range(NT):
                g, j = divmod(t, 4)
                act.wait_ge(norm_ok, g + 1)
                a.activation(big[:, t, :], big[:, t, :], ACT.Identity, bias=lnb[:, g, j:j + 1],
                             scale=lna[:, g, j:j + 1]).then_inc(xn_ok, 1)
            for e in range(E):
                act.wait_ge(exp_in[e % 2], 16 * (e // 2 + 1))
                copy(wr[:, HI, e * EW:(e + 1) * EW], stream[:, e % 2, :]).then_inc(exp_hi, 1)
            act.wait_ge(vw_mm, 2)
            for dt in range(DT):
                a.activation(vw[:, HI, dt, :], bank[2 + dt // 2][:, 256 * (dt % 2):256 * (dt % 2) + 256],
                             ACT.Copy, scale=lns[:, 0, dt:dt + 1]).then_inc(vw_hi, 1)

            def x_high(i, first=False):
                act.wait_ge(x_turned, i + 1)
                if not first:
                    act.wait_ge(h_done, i)
                copy(xTs[:, HI, :], bank[4][:, :]).then_inc(xt_hi, 1)

            def silu(i, first=False):
                act.wait_ge(h_done, i + 1)
                if not first:
                    act.wait_ge(h_gated, i)
                a.activation(sil[:, :], bank[5][:, :], ACT.Silu).then_inc(h_silu, 1)

            def act_high(i, first=False):
                act.wait_ge(a_turned, i + 1)
                if not first:
                    act.wait_ge(y_done, i)
                copy(aTs[:, HI, :], bank[6][:, :]).then_inc(at_hi, 1)

            def copy_y(i, first=False):
                act.wait_ge(y_done, i + 1)
                if first:
                    act.wait_ge(tail_ok, 16)
                else:
                    act.wait_ge(y_stored, i * 16)
                copy(ysb[:, :], bank[7][:, :]).then_inc(y_copied, 1)

            x_high(0, first=True)
            silu(0, first=True)
            x_high(1)
            act_high(0, first=True)
            silu(1)
            x_high(2)
            copy_y(0, first=True)
            act_high(1)
            with act.Fori(2, ITEMS - 1) as i:
                silu(i)
                x_high(i + 1)
                copy_y(i - 1)
                act_high(i)
            last = ITEMS - 1
            silu(last)
            copy_y(last - 1)
            act_high(last)
            copy_y(last)

            def split_wqk(b, q):
                copy(wqs[:, HI, :, :, :], wqk_v[:, :, :, bass.ds(q * P, P)]).then_inc(wq_hi, 1)

            def split_qk(b, q, which, first=False):
                n = b * NQ + q
                act.wait_ge(qk_done, n * 2 + which + 1)
                if which == 0 and not first:
                    for k in range(2):
                        act.wait_ge(stk[k], n * 96)
                copy(qk[:, (Q_HI, K_HI)[which], :], bank[QKB][:, :]).then_inc(qk_hi, 1)

            def exponentials(n, par):
                for qt, maxima in ((3, 1), (2, 3), (0, 3), (1, 4)):
                    act.wait_ge(nb_ok, n * 4 + maxima)
                    bk, col, at = SCORE[qt]
                    w = P * (qt + 1)
                    a.activation(prob[par][:, at:at + w], bank[bk][:, col:col + w], ACT.Exp,
                                 bias=nb[:, qt:qt + 1], accum_out=rs[:, par, qt:qt + 1]).then_inc(exp_ok, 1)

            def head_step(b, q, j, one_more=True):
                n = (b * NQ + q) * QH + j
                if one_more:
                    exponentials(n + 1, (j + 1) % 2)
                if j == 0:
                    act.wait_ge(pv_done, b + 1 + n)
                    act.wait_ge(vp_copied, b * 2 + 2)
                    act.wait_ge(vst_zero, 1)
                    copy(vst_v[:, :, :, 0:R], vp[:, :, bass.ds(q * QH, QH), :]).then_inc(vst_hi, 1)
                for i, (bk, w, at) in enumerate(((4, 512, 0), (5, 512, 512), (6, 256, 1024))):
                    act.wait_ge(p_turned, n * 3 + i + 1)
                    copy(pts[:, j % 2, HI, at:at + w], bank[bk][:, 0:w]).then_inc(pt_hi, 1)

            def quad(b, q, ahead):
                for j in range(QH):
                    head_step(b, q, j, ahead or j < QH - 1)
                    if j == 0 and ahead:
                        split_qk(b, q + 1, 1)
                    if j == 1 and ahead == 2:
                        split_wqk(b, q + 2)
                    if j == 3 and ahead == 2:
                        split_qk(b, q + 2, 0)

            def split_gate_up(b, c, par):
                act.wait_ge(cg_in[par], loads_of(b, c))
                raw, dst = gu_view(stream[:, par, 0:CW]), gu_view(wch[:, par, HI, 0:CW])
                for dt in range(DT):
                    ins = a.activation(dst[:, :, dt, :], raw[:, :, dt, :], ACT.Copy, scale=lns[:, 1, dt:dt + 1])
                ins.then_inc(cg_hi, 1)

            def chunk_step(b, c, par, more=True):
                n = b * NCH + c
                act.wait_ge(g_done, n + 1)
                a.activation(sil[:, :], bank[GATE][:, :], ACT.Silu).then_inc(g_silu, 1)
                act.wait_ge(cd_in[par], loads_of(b, c))
                copy(wch[:, par, HI, CW:CW + D], stream[:, par, CW:CW + D]).then_inc(cd_hi, 1)
                act.wait_ge(gu_ok, n + 1)
                copy(actr[:, par, HI, :], act_sb[:, :]).then_inc(gu_hi, 1)
                if more:
                    split_gate_up(b, c + 2, par)

            act.wait_ge(y_done, ITEMS)
            with act.Fori(0, NB) as b:
                for j in range(TT):
                    act.wait_ge(ln_ok, b + 1)
                    a.activation(hb[:, j, :], xt[:, j, :], ACT.Identity, bias=lnb[:, 0, j:j + 1],
                                 scale=lna[:, 0, j:j + 1]).then_inc(hb_ok, 1)
                for dt in range(DT):
                    act.wait_ge(hb_turned, b * 4 + dt + 1)
                    copy(hT[:, HI, dt, :], bank[dt][:, :]).then_inc(ht_hi, 1)
                act.wait_ge(wqk_ok, 1)
                split_wqk(b, 0)
                for k in range(2):
                    act.wait_ge(vp_done, b * 2 + k + 1)
                    copy(vp[:, 2 * k:2 * k + 2, :, :].rearrange("p t h r -> p (t h r)"),
                         bank[4 + k][:, :]).then_inc(vp_copied, 1)
                act.wait_ge(ha_done, b + 1)
                copy(att_low, bank[6][32:32 + R, :]).then_inc(ha_low, 1)
                for which in range(2):
                    split_qk(b, 0, which, first=True)
                act.wait_ge(bst_ok, 2)
                split_wqk(b, 1)
                exponentials(b * H, 0)
                split_qk(b, 1, 0)
                with act.Fori(0, NQ - 2) as q:
                    quad(b, q, 2)
                quad(b, NQ - 2, 1)
                quad(b, NQ - 1, 0)
                for par in range(2):
                    split_gate_up(b, par, par)
                act.wait_ge(pv_done, (b + 1) * (H + 1))
                copy(att_low, bank[ATT][32:32 + R, :]).then_inc(at_low, 1)
                act.wait_ge(at_sum, b + 1)
                a.activation(att_low, att_sum, ACT.Tanh).then_inc(mod_ok, 1)
                act.wait_ge(z_ok, b + 1)
                copy(zst[0:R, :], zrow)
                copy(zst[64:64 + R, :], zrow).then_inc(zs_hi, 1)
                with act.Fori(0, NCH // 2 - 1) as c2:
                    chunk_step(b, c2 * 2, 0)
                    chunk_step(b, c2 * 2 + 1, 1)
                chunk_step(b, NCH - 2, 0, more=False)
                chunk_step(b, NCH - 1, 1, more=False)

        @block.vector
        def _(dve):
            v = nc.vector
            own = [0]

            def step(ins):
                own[0] += 1
                return ins.then_inc(dve_own, 1)

            def settle():
                dve.wait_ge(dve_own, own[0])

            def link(ins):
                step(ins)
                settle()

            step(v.memset(ge[:, 0, :], 1.0))
            step(v.memset(ge[:, E, :], 0.0))
            step(v.memset(small[:, :, :], 0.0))
            dve.wait_ge(ids_in, 16)
            link(v.tensor_copy(idf[:, :], idst[:, :]))
            for e in range(1, E):
                step(v.tensor_scalar(ge[:, e, :], idf[:, :], float(e * PER_EXPERT), None, ALU.is_ge))
            settle()
            v.tensor_tensor(oh[:, :, :], ge[:, 0:E, :], ge[:, 1:E + 1, :], ALU.subtract).then_inc(onehot_ok, 1)
            dve.wait_ge(ranks_ok, 1)
            dve.wait_ge(onehot_ok, 1)
            link(v.tensor_copy(cnt[:, :, :].rearrange("p a b -> p (a b)"), bank[0][:, 0:2 * E * NT]))
            total = cnt[:, 1, :]
            dve.wait_ge(const_ok, 6)
            link(v.tensor_tensor_scan(cum[:, :], ones[:, 0:E * NT], total, 0.0, ALU.mult, ALU.add))
            link(v.tensor_tensor(exc[:, :], cum[:, :], total, ALU.subtract))
            pef = pe_[:, :, :].rearrange("p e t -> p (e t)")
            link(v.tensor_tensor(pef, exc[:, :], cnt[:, 0, :], ALU.add))
            link(v.tensor_tensor(pef, pef, oh[:, :, :].rearrange("p e t -> p (e t)"), ALU.mult))
            link(v.tensor_reduce(posf[:, :], pe_[:, :, :].rearrange("p e t -> p t e"), AXX, ALU.add))
            v.tensor_copy(pos[:, :], posf[:, :]).then_inc(pos_ok, 1)
            OFF, CNT, NTF, TIN, TEX, DD, DIF = range(7)
            off, excv, cumv = small[:, OFF, :], exc[:, :].rearrange("p (e t) -> p e t", e=E), cum[:, :].rearrange("p (e t) -> p e t", e=E)
            link(v.tensor_copy(off, excv[:, :, 0]))
            link(v.tensor_tensor(small[:, CNT, :], cumv[:, :, NT - 1], off, ALU.subtract))
            link(v.tensor_scalar(nti[:, :], small[:, CNT, :], float(P - 1), None, ALU.add))
            link(v.tensor_scalar(nti[:, :], nti[:, :], P.bit_length() - 1, None, ALU.logical_shift_right))
            link(v.tensor_copy(small[:, NTF, :], nti[:, :]))
            link(v.tensor_tensor_scan(small[:, TIN, :], ones[:, 0:E], small[:, NTF, :], 0.0, ALU.mult, ALU.add))
            link(v.tensor_tensor(small[:, TEX, :], small[:, TIN, :], small[:, NTF, :], ALU.subtract))
            link(v.scalar_tensor_tensor(out=small[:, DD, :], in0=small[:, TEX, :], scalar=-float(P), in1=off,
                                        op0=ALU.mult, op1=ALU.add))
            link(v.tensor_tensor(small[:, DIF, 1:E], small[:, DD, 1:E], small[:, DD, 0:E - 1], ALU.subtract))
            step(v.tensor_scalar(its[:, 0, :], itf[:, :], float(P), None, ALU.mult))
            step(v.memset(its[:, 1, :], 0.0))
            settle()
            for e in range(1, E):
                edge = small[:, TEX, e:e + 1]
                step(v.tensor_scalar(its[:, 2, :], itf[:, :], edge, small[:, DIF, e:e + 1], ALU.is_ge, ALU.mult))
                link(v.scalar_tensor_tensor(out=its[:, 1, :], in0=itf[:, :], scalar=edge, in1=its[:, 1, :],
                                            op0=ALU.is_ge, op1=ALU.add))
                link(v.tensor_tensor(its[:, 0, :], its[:, 0, :], its[:, 2, :], ALU.add))
            step(v.tensor_scalar(itab[:, 0, :], its[:, 0, :], float(T), None, ALU.min))
            step(v.tensor_scalar(itab[:, 1, :], its[:, 1, :], float(EW), None, ALU.mult))
            dve.wait_ge(dve_own, own[0])
            v.tensor_copy(small[:, 15, :], small[:, DD, :]).then_inc(items_ok, 1)

            def statistics(rows, mark, done):
                for j in range(4):
                    mark(v.bn_stats(st[:, j, :], rows[:, j, :]))
                done()
                mark(v.memset(nr[:, 9, :], 0.0))
                for j in range(4):
                    mark(v.bn_aggr(mv[:, j, :], st[:, j, :]))
                done()

            def inverse_root(dst, x_, mark, done):
                mark(v.tensor_scalar(nri[:, 0, :], x_.bitcast(I32), 1, None, ALU.arith_shift_right))
                done()
                mark(v.tensor_scalar(dst.bitcast(I32), nri[:, 0, :], -1.0, float(0x5F3759DF), ALU.mult, ALU.add))
                done()
                for _ in range(3):
                    mark(v.tensor_tensor(nr[:, 10, :], dst, dst, ALU.mult))
                    done()
                    mark(v.tensor_tensor(nr[:, 11, :], nr[:, 10, :], x_, ALU.mult))
                    done()
                    mark(v.tensor_scalar(nr[:, 10, :], nr[:, 11, :], -0.5, 1.5, ALU.mult, ALU.add))
                    done()
                    mark(v.tensor_tensor(dst, dst, nr[:, 10, :], ALU.mult))
                    done()

            VE, R1, V2, R2, SM, T1, T2 = range(7)
            mean, var = mv[:, :, 0], mv[:, :, 1]
            for g in range(4):
                dve.wait_ge(x_in[g], 16)
                statistics(big[:, 4 * g:4 * g + 4, :], step, settle)
                link(v.tensor_scalar(nr[:, VE, :], var, LN_EPS, None, ALU.add))
                inverse_root(nr[:, R1, :], nr[:, VE, :], step, settle)
                step(v.tensor_copy(lna[:, g, :], nr[:, R1, :]))
                link(v.scalar_tensor_tensor(out=lnb[:, g, :], in0=mean, scalar=-1.0, in1=nr[:, R1, :],
                                            op0=ALU.mult, op1=ALU.mult))
                v.tensor_copy(nr[:, T1, :], nr[:, R1, :]).then_inc(norm_ok, 1)

            for e in range(E):
                dve.wait_ge(exp_hi, e + 1)
                v.tensor_tensor(wr[:, LO, e * EW:(e + 1) * EW], stream[:, e % 2, :],
                                wr[:, HI, e * EW:(e + 1) * EW].bitcast(F32), ALU.subtract).then_inc(exp_lo, 1)
                if e == 0:
                    link(v.memset(bd[:, :, :, :], 0.0))
                    dve.wait_ge(woa_ok, 1)
                    woa = bank[1][:, 0:DT * R].rearrange("p (c r) -> p c r", c=DT)
                    for h in range(QH):
                        rows = slice(HD * h, HD * h + HD)
                        ins = v.tensor_copy(bd[rows, :, h, :], woa[rows, :, :])
                    ins.then_inc(bd_ok, 1)
            dve.wait_ge(vw_hi, DT)
            for dt in range(DT):
                ins = v.scalar_tensor_tensor(
                    out=vw[:, LO, dt, :], in0=bank[2 + dt // 2][:, 256 * (dt % 2):256 * (dt % 2) + 256],
                    scalar=lns[:, 0, dt:dt + 1], in1=vw[:, HI, dt, :].bitcast(F32), op0=ALU.mult, op1=ALU.subtract)
            ins.then_inc(prep_ok, 1)

            def x_low(i):
                dve.wait_ge(xt_hi, i + 1)
                v.tensor_tensor(xTs[:, LO, :], bank[4][:, :], xTs[:, HI, :].bitcast(F32),
                                ALU.subtract).then_inc(xt_lo, 1)

            def gated(i):
                dve.wait_ge(h_silu, i + 1)
                v.tensor_tensor(act_sb[:, :], bank[5][:, :], sil[:, :], ALU.mult).then_inc(h_gated, 1)

            def act_low(i):
                dve.wait_ge(at_hi, i + 1)
                v.tensor_tensor(aTs[:, LO, :], bank[6][:, :], aTs[:, HI, :].bitcast(F32),
                                ALU.subtract).then_inc(at_lo, 1)

            x_low(0)
            gated(0)
            x_low(1)
            act_low(0)
            with dve.Fori(1, ITEMS - 1) as i:
                gated(i)
                x_low(i + 1)
                act_low(i)
            gated(ITEMS - 1)
            act_low(ITEMS - 1)

            dve.wait_ge(wqk_in, 16)
            for dt in range(DT):
                v.tensor_scalar(wqk_v[:, 0, dt, :], wqk_v[:, 0, dt, :], lns[:, 0, dt:dt + 1], SCALE, ALU.mult, ALU.mult)
                ins = v.tensor_scalar(wqk_v[:, 1, dt, :], wqk_v[:, 1, dt, :], lns[:, 0, dt:dt + 1], None, ALU.mult)
            ins.then_inc(wqk_ok, 1)
            dve.wait_ge(y_done, ITEMS)
            v.memset(vst.bitcast(F32), 0.0).then_inc(vst_zero, 1)
            v.memset(zst[:, :].bitcast(F32), 0.0).then_inc(vst_zero, 1)

            def low(dst, src, high, done):
                v.tensor_tensor(dst, src, high.bitcast(F32), ALU.subtract).then_inc(done, 1)

            def wqk_low(b, q):
                dve.wait_ge(wq_hi, b * NQ + q + 1)
                low(wqs[:, LO, :, :, :], wqk_v[:, :, :, bass.ds(q * P, P)], wqs[:, HI, :, :, :], wq_lo)

            def qk_low(b, q, which):
                dve.wait_ge(qk_hi, (b * NQ + q) * 2 + which + 1)
                low(qk[:, (Q_LO, K_LO)[which], :], bank[QKB][:, :], qk[:, (Q_HI, K_HI)[which], :], qk_lo)

            def maxima(n):
                for i, qts in enumerate(((3,), (2, 0), (1,))):
                    dve.wait_ge(s_done, n * 3 + i + 1)
                    for qt in qts:
                        bk, col, _ = SCORE[qt]
                        v.reduce_max(nb[:, qt:qt + 1], bank[bk][:, col:col + P * (qt + 1)], AXX,
                                     negate=True).then_inc(nb_ok, 1)

            def normalise(n, par):
                dve.wait_ge(exp_ok, n * 4 + 4)
                v.reciprocal(rr[:, :], rs[:, par, :]).then_inc(rr_ok, 1)
                dve.wait_ge(rr_ok, n + 1)
                for qt in (3, 2, 0, 1):
                    at = SCORE[qt][2]
                    rows = prob[par][:, at:at + P * (qt + 1)]
                    v.tensor_scalar(rows, rows, rr[:, qt:qt + 1], None, ALU.mult).then_inc(pn_ok, 1)

            def head_step(b, q, j, two_more=True, one_more=True):
                n = (b * NQ + q) * QH + j
                if one_more:
                    normalise(n + 1, (j + 1) % 2)
                if two_more:
                    maxima(n + 2)
                if j == 0:
                    dve.wait_ge(vst_hi, b * NQ + q + 1)
                    low(vst_v[:, :, :, 32:32 + R], vp[:, :, bass.ds(q * QH, QH), :], vst_v[:, :, :, 0:R], vst_lo)
                for i, (bk, w, at) in enumerate(((4, 512, 0), (5, 512, 512), (6, 256, 1024))):
                    dve.wait_ge(pt_hi, n * 3 + i + 1)
                    low(pts[:, j % 2, LO, at:at + w], bank[bk][:, 0:w], pts[:, j % 2, HI, at:at + w], pt_lo)

            def quad(b, q, ahead):
                last = ahead == 0
                for j in range(QH):
                    head_step(b, q, j, not last or j < QH - 2, not last or j < QH - 1)
                    if j == 0 and ahead:
                        qk_low(b, q + 1, 1)
                    if j == 1 and ahead == 2:
                        wqk_low(b, q + 2)
                    if j == 3 and ahead == 2:
                        qk_low(b, q + 2, 0)

            def gate_up_low(b, c, par):
                dve.wait_ge(cg_hi, b * NCH + c + 1)
                raw, high, dst = (gu_view(t) for t in (stream[:, par, 0:CW], wch[:, par, HI, 0:CW], wch[:, par, LO, 0:CW]))
                for dt in range(DT):
                    ins = v.scalar_tensor_tensor(out=dst[:, :, dt, :], in0=raw[:, :, dt, :], scalar=lns[:, 1, dt:dt + 1],
                                                 in1=high[:, :, dt, :].bitcast(F32), op0=ALU.mult, op1=ALU.subtract)
                v.tensor_copy(bchunk[:, par, :], bst[:, bass.ds(c * P, P)].bitcast(F32)).then_inc(cg_lo, 1)

            def down_low(b, c, par):
                dve.wait_ge(cd_hi, b * NCH + c + 1)
                low(wch[:, par, LO, CW:CW + D], stream[:, par, CW:CW + D], wch[:, par, HI, CW:CW + D], cd_lo)

            def chunk_step(b, c, par, more=True):
                n = b * NCH + c
                down_low(b, c, par)
                dve.wait_ge(g_silu, n + 1)
                dve.wait_ge(u_done, n + 1)
                v.tensor_tensor(act_sb[:, :], bank[UP][:, :], sil[:, :], ALU.mult).then_inc(gu_ok, 1)
                dve.wait_ge(gu_hi, n + 1)
                low(actr[:, par, LO, :], act_sb[:, :], actr[:, par, HI, :], gu_lo)
                if more:
                    gate_up_low(b, c + 2, par)
                dve.wait_ge(gu_lo, n + 1)

            K_LN = 54
            with dve.Fori(0, NB) as b:
                mine = [0]

                def mark(ins):
                    mine[0] += 1
                    ins.then_inc(ln_own, 1)

                def done():
                    dve.wait_ge(ln_own, b * K_LN + mine[0])

                dve.wait_ge(xt_in, b * 16 + 16)
                dve.wait_ge(y_in, (b + 1) * 16 * TT)
                dve.wait_ge(tanh_ok, 1)
                for j in range(TT):
                    mark(v.scalar_tensor_tensor(out=xt[:, j, :], in0=hb[:, j, :], scalar=tg[:, 0:1], in1=xt[:, j, :],
                                                op0=ALU.mult, op1=ALU.add))
                done()
                statistics(xt, mark, done)
                mark(v.tensor_scalar(nr[:, VE, :], var, LN_EPS, None, ALU.add))
                done()
                inverse_root(nr[:, R1, :], nr[:, VE, :], mark, done)
                mark(v.tensor_tensor(nr[:, T1, :], nr[:, R1, :], nr[:, R1, :], ALU.mult))
                done()
                mark(v.tensor_tensor(nr[:, V2, :], nr[:, T1, :], var, ALU.mult))
                done()
                mark(v.tensor_scalar(nr[:, V2, :], nr[:, V2, :], RMS_EPS, None, ALU.add))
                done()
                inverse_root(nr[:, R2, :], nr[:, V2, :], mark, done)
                mark(v.tensor_tensor(lna[:, 0, :], nr[:, R1, :], nr[:, R2, :], ALU.mult))
                done()
                mark(v.scalar_tensor_tensor(out=lnb[:, 0, :], in0=mean, scalar=-1.0, in1=lna[:, 0, :],
                                            op0=ALU.mult, op1=ALU.mult))
                mark(v.tensor_scalar(nr[:, T1, :], nr[:, R1, :], tg[:, 1:2], None, ALU.mult))
                done()
                mark(v.scalar_tensor_tensor(out=nr[:, T2, :], in0=mean, scalar=-1.0, in1=nr[:, T1, :],
                                            op0=ALU.mult, op1=ALU.mult))
                mark(v.tensor_scalar(nr[:, SM, :], nr[:, T1, :], 1.0, None, ALU.add))
                done()
                v.tensor_copy(nr[:, VE, :], nr[:, T2, :]).then_inc(ln_ok, 1)
                for j in range(TT):
                    dve.wait_ge(hb_ok, b * 4 + j + 1)
                    mark(v.tensor_scalar(xt[:, j, :], xt[:, j, :], nr[:, SM, j:j + 1], nr[:, T2, j:j + 1],
                                         ALU.mult, ALU.add))
                assert mine[0] == K_LN, mine[0]
                for dt in range(DT):
                    dve.wait_ge(ht_hi, b * 4 + dt + 1)
                    low(hT[:, LO, dt, :], bank[dt][:, :], hT[:, HI, dt, :], ht_lo)
                wqk_low(b, 0)
                dve.wait_ge(ha_low, b + 1)
                v.tensor_tensor(haT, bank[6][0:R, :], att_low, ALU.add).then_inc(ha_ok, 1)
                for which in range(2):
                    qk_low(b, 0, which)
                maxima(b * H)
                wqk_low(b, 1)
                normalise(b * H, 0)
                maxima(b * H + 1)
                qk_low(b, 1, 0)
                with dve.Fori(0, NQ - 2) as q:
                    quad(b, q, 2)
                quad(b, NQ - 2, 1)
                quad(b, NQ - 1, 0)
                for par in range(2):
                    gate_up_low(b, par, par)
                dve.wait_ge(at_low, b + 1)
                v.tensor_tensor(att_sum, bank[ATT][0:R, :], att_low, ALU.add).then_inc(at_sum, 1)
                dve.wait_ge(mod_ok, b + 1)
                v.scalar_tensor_tensor(out=zrow, in0=att_low, scalar=MOD_SCALE, in1=haT,
                                       op0=ALU.mult, op1=ALU.mult).then_inc(z_ok, 1)
                dve.wait_ge(zs_hi, b + 1)
                low(zst[32:32 + R, :], zrow, zst[0:R, :], zs_ok)
                with dve.Fori(0, NCH // 2 - 1) as c2:
                    chunk_step(b, c2 * 2, 0)
                    chunk_step(b, c2 * 2 + 1, 1)
                chunk_step(b, NCH - 2, 0, more=False)
                chunk_step(b, NCH - 1, 1, more=False)
                dve.wait_ge(d_done, (b + 1) * NCH)
                dve.wait_ge(ln_own, (b + 1) * K_LN)
                for tt in range(TT):
                    ins = v.scalar_tensor_tensor(out=xt[:, tt, :], in0=bank[Y0 + tt][:, :], scalar=tg[:, 1:2],
                                                 in1=xt[:, tt, :], op0=ALU.mult, op1=ALU.add)
                ins.then_inc(fin_out, 1)


def kernel(x, itok_BxS_13_99985, ctx_2048, g_xattn, g_ffn, L0_ffn_ln1_w, L0_ffn_ln2_w, L0_ffn_Wq, L0_ffn_Wk,
           L0_ffn_Wv, L0_ffn_Wo, L0_ffn_A, L0_ffn_B, L0_ffn_W_in_base, L0_ffn_W_up_base, L0_ffn_W_down):
    import concourse.bacc as bacc
    import numpy as np
    from concourse.bass_utils import run_bass_kernel_spmd

    def c(a):
        return np.ascontiguousarray(a)

    def by_row(w):
        w = np.asarray(w)
        return w.reshape(-1, P, w.shape[-1]).transpose(1, 0, 2).reshape(P, -1)

    ctx_2048 = np.asarray(ctx_2048)
    wi, wu = (np.asarray(w).reshape(NCH, P, DT, P).transpose(3, 0, 2, 1).reshape(P, NCH, DT * P)
              for w in (L0_ffn_W_in_base, L0_ffn_W_up_base))
    wd = np.asarray(L0_ffn_W_down).T.reshape(NCH, P, D).transpose(1, 0, 2)
    arrays = {
        "x": c(np.asarray(x).reshape(T, D)),
        "ids": c(np.asarray(itok_BxS_13_99985).reshape(NT, P).T),
        "wexp": c(np.stack([by_row(ctx_2048[e].T) for e in range(E)], 1)),
        "wov": c(np.stack([by_row(L0_ffn_Wo), by_row(L0_ffn_Wv)], 1)),
        "amat": c(by_row(L0_ffn_A).reshape(P, DT, R)),
        "bmat": c(np.asarray(L0_ffn_B)),
        "ln": c(np.stack([np.asarray(w).reshape(DT, P).T for w in (L0_ffn_ln1_w, L0_ffn_ln2_w)], 1)),
        "gates": c(np.stack([np.asarray(g_xattn), np.asarray(g_ffn)], 1)),
        "wqk": c(np.stack([by_row(np.asarray(w).T) for w in (L0_ffn_Wq, L0_ffn_Wk)], 1)),
        "wmlp": c(np.concatenate([wi, wu, wd], 2)),
    }
    nc = bacc.Bacc("TRN2", target_bir_lowering=False, num_devices=1)
    args = {n: nc.dram_tensor(f"in_{n}", a.shape, mybir.dt.from_np(a.dtype), kind="ExternalInput").ap()
            for n, a in arrays.items()}
    out = nc.dram_tensor("out", [T, D], F32, kind="ExternalOutput").ap()
    build(nc, **args, out=out)
    got = run_bass_kernel_spmd(nc, [{f"in_{n}": a for n, a in arrays.items()}], core_ids=[0]).results[0]["out"]
    return got.reshape(NB, S, D)
```

```python
from contextlib import ExitStack

import concourse.bass as bass
from concourse import mybir

F32 = mybir.dt.float32
F32R = mybir.dt.float32r
I32 = mybir.dt.int32
ALU = mybir.AluOpType
ACT = mybir.ActivationFunctionType
AXX = mybir.AxisListType.X

P = 128
NB, S, D = 4, 512, 512
T = NB * S
DT = D // P
TT = S // P
NT = T // P
E = 4
PER_EXPERT = 25000 // E
ITEMS = T // P + E - 1
EW = DT * D
H, HD, R = 16, 32, 16
QH = P // HD
NQ = H // QH
F = 2048
NCH = F // P
CW = 2 * DT * P
LN_EPS, RMS_EPS = 1e-5, 1e-6
MASKED = -1e30
SCALE = float(HD) ** -0.5
MOD_SCALE = 0.1
HI, LO = 0, 1
Q_LO, Q_HI, K_HI, K_LO = range(4)
GATE, UP, Y0, QKB, ATT = 0, 1, 2, 3, 7
SCORE = {3: (0, 0, 0), 2: (1, 0, 512), 0: (1, 384, 896), 1: (2, 0, 1024)}
ROWS = (6, 7, 0, 1)
VALUES, LOW_RANK = (6, 7), 0
TURNED = {0: (4, 0, 0), 1: (5, 0, 512), 3: (5, 384, 896), 2: (6, 0, 1024)}
PACKED = 1280
K_LN = 2 * TT + (13 + 12) + TT
NORM_AT = 4
PARTS = ((HI, HI), (LO, HI), (HI, LO))


def build(nc, x, ids, wexp, wov, amat, bmat, ln, gates, wqk, wmlp, out):
    ctx = ExitStack()
    with ctx:
        def sb(name, shape, dt=F32):
            return ctx.enter_context(nc.sbuf_tensor(name, shape, dt))

        def sem(name):
            return ctx.enter_context(nc.semaphore(name))

        xs = nc.dram_tensor("x_sorted", [T + P, D], F32).ap()
        res = nc.dram_tensor("residual", [T, D], F32).ap()
        ys = nc.dram_tensor("y_sorted", [T + P, D], F32).ap()

        big = sb("big", [P, NT, D])
        xt = big[:, 0:4, :]
        hb = big[:, 4:8, :]
        flat = big[:, :, :].rearrange("p a b -> p (a b)")
        x1 = big[:, 8:12, :]
        x1f = flat[:, 4096:4096 + TT * D]
        hbf = flat[:, 2048:2048 + TT * D]
        prob = [flat[:, 4096 + PACKED * k:4096 + PACKED * (k + 1)] for k in range(2)]
        vp = flat[:, 6656:6656 + TT * H * R].rearrange("p (t h r) -> p t h r", t=TT, h=H)
        stream = sb("stream", [P, 2, EW])
        wstage = sb("wstage", [P, 2, EW])
        wr = sb("wr", [P, 2, E * EW], F32R)
        wrf = wr[:, :, :].rearrange("p a b -> p (a b)")

        def carve(start, n):
            return wrf[:, start:start + n]

        hT = carve(0, 4096).rearrange("p (a d t) -> p a d t", a=2, d=DT)
        wqs = carve(4096, 2048).rearrange("p (a m d c) -> p a m d c", a=2, m=2, d=DT)
        qk = carve(6144, 2048).rearrange("p (m t) -> p m t", m=4)
        pts = carve(8192, 4 * PACKED).rearrange("p (h a c) -> p h a c", h=2, a=2)
        VS = QH * 64 + 64
        vst = carve(8192 + 4 * PACKED, TT * VS).rearrange("p (t c) -> p t c", t=TT)
        vst_v = vst[:, :, 0:QH * 64].rearrange("p t (h c) -> p t h c", h=QH)
        wqk_v = wstage[:, :, :].rearrange("p m (d c) -> p m d c", d=DT)
        braw = flat[0:96, 6144:6144 + F]
        stack = sb("stack", [3 * HD, 2, 2, S], F32R)
        vw = sb("vw", [P, 2, DT, H * R], F32R)
        apad = sb("apad", [P, DT, P], F32R)
        zst = sb("zst", [96, S], F32R)
        bst = sb("bst", [96, F], F32R)
        identr = sb("identr", [P, P], F32R)
        maskr = sb("maskr", [P, P], F32R)
        zeror = sb("zeror", [P, P], F32R)
        wch = sb("wch", [P, 2, 2, CW + D], F32R)
        actr = sb("actr", [P, 2, 2, S], F32R)
        xTs, aTs = actr[:, 0], actr[:, 1]
        ident = sb("ident", [P, P])
        tri = sb("tri", [P, P])
        ones = sb("ones", [P, P])
        xi = sb("xi", [P, D])
        sil = sb("sil", [P, S])
        act_sb = sb("act_sb", [P, S])
        ysb = sb("ysb", [P, D])
        araw = sb("araw", [P, DT, R])
        lns = sb("lns", [P, 2, DT])
        gt = sb("gt", [P, 2])
        tg = sb("tg", [P, 2])
        bd = sb("bd", [P, DT, QH, R])
        idst = sb("idst", [P, NT], I32)
        idf = sb("idf", [P, NT])
        ge = sb("ge", [P, E + 1, NT])
        oh = sb("oh", [P, E, NT])
        cnt = sb("cnt", [P, 2, E * NT])
        cum = sb("cum", [P, E * NT])
        exc = sb("exc", [P, E * NT])
        pe_ = sb("pe_", [P, E, NT])
        posf = sb("posf", [P, NT])
        pos = sb("pos", [P, NT], I32)
        small = sb("small", [P, 16, E])
        lna = sb("lna", [P, NT])
        lnb = sb("lnb", [P, NT])
        bchunk = sb("bchunk", [96, 2, P], F32R)
        asc = sb("asc", [P, DT, R])
        nti = sb("nti", [P, E], I32)
        itf = sb("itf", [P, 20])
        its = sb("its", [P, 3, 20])
        itab = sb("itab", [P, 2, 20], I32)
        st = sb("st", [P, 8 * 6])
        mv = sb("mv", [P, 8, 2])
        nr = sb("nr", [P, 8 * 8])
        nri = sb("nri", [P, 8], I32)
        nb = sb("nb", [P, 4])
        rs = sb("rs", [P, 2, 4])
        rr = sb("rr", [P, 4])
        haT, att_low, att_sum, zrow = xi[0:R, :], ysb[0:R, :], act_sb[0:R, :], sil[0:R, :]

        bank = [ctx.enter_context(nc.psum_tensor(f"bank{k}", [P, 512], F32)) for k in range(8)]

        ids_in, small_in, wov_in, wqk_in = sem("ids_in"), sem("small_in"), sem("wov_in"), sem("wqk_in")
        b_in = sem("b_in")
        x_in = [sem(f"x_in{g}") for g in range(4)]
        exp_in = [sem(f"exp_in{k}") for k in range(2)]
        exp_hi, exp_lo = sem("exp_hi"), sem("exp_lo")
        const_ok, zero_ok, tail_ok = sem("const_ok"), sem("zero_ok"), sem("tail_ok")
        pool_own, dve_own, act_own = sem("pool_own"), sem("dve_own"), sem("act_own")
        onehot_ok, ranks_ok, pos_ok, items_ok = sem("onehot_ok"), sem("ranks_ok"), sem("pos_ok"), sem("items_ok")
        norm_ok, xn_ok, scattered = sem("norm_ok"), sem("xn_ok"), sem("scattered")
        woa_ok, bd_ok, vw_mm, vw_hi, prep_ok = sem("woa_ok"), sem("bd_ok"), sem("vw_mm"), sem("vw_hi"), sem("prep_ok")
        tanh_ok, wqk_ok = sem("tanh_ok"), sem("wqk_ok")
        a_hi, b_hi = sem("a_hi"), sem("b_hi")
        xi_in, x_turned, xt_hi, xt_lo = sem("xi_in"), sem("x_turned"), sem("xt_hi"), sem("xt_lo")
        h_done, h_silu, h_gated = sem("h_done"), sem("h_silu"), sem("h_gated")
        a_turned, at_hi, at_lo = sem("a_turned"), sem("at_hi"), sem("at_lo")
        y_done, y_copied, y_stored = sem("y_done"), sem("y_copied"), sem("y_stored")
        x1_in, y_in, res_out, res_in = sem("x1_in"), sem("y_in"), sem("res_out"), sem("res_in")
        ln_ok, hb_ok, fin_ok = sem("ln_ok"), sem("hb_ok"), sem("fin_ok")
        hb_turned, ht_hi, ht_lo = sem("hb_turned"), sem("ht_hi"), sem("ht_lo")
        vp_done, vp_copied = sem("vp_done"), sem("vp_copied")
        ha_done, ha_low, ha_ok = sem("ha_done"), sem("ha_low"), sem("ha_ok")
        wq_hi, wq_lo = sem("wq_hi"), sem("wq_lo")
        qk_done, qk_hi, qk_lo = sem("qk_done"), sem("qk_hi"), sem("qk_lo")
        stk = [sem(f"stk{k}") for k in range(2)]
        vst_hi, vst_lo = sem("vst_hi"), sem("vst_lo")
        s_done, nb_ok, exp_ok, pn_ok = sem("s_done"), sem("nb_ok"), sem("exp_ok"), sem("pn_ok")
        p_turned, pt_hi, pt_lo, pv_done = sem("p_turned"), sem("pt_hi"), sem("pt_lo"), sem("pv_done")
        at_low, at_sum, mod_ok, z_ok, zs_hi, zs_ok = (sem(n) for n in ("at_low", "at_sum", "mod_ok", "z_ok", "zs_hi", "zs_ok"))
        cg_in = [sem(f"cg_in{k}") for k in range(2)]
        cd_in = [sem(f"cd_in{k}") for k in range(2)]
        cg_hi, cg_lo, cd_hi, cd_lo = (sem(n) for n in ("cg_hi", "cg_lo", "cd_hi", "cd_lo"))
        apad_ok, bst_ok, vst_zero, rr_ok, ln_own = (sem(n) for n in ("apad_ok", "bst_ok", "vst_zero", "rr_ok", "ln_own"))
        g_done, u_done, g_silu, gu_ok, gu_hi, gu_lo = (sem(n) for n in ("g_done", "u_done", "g_silu", "gu_ok", "gu_hi", "gu_lo"))
        d_done, fin_out, out_in = sem("d_done"), sem("fin_out"), sem("out_in")

        def gu_view(cols):
            return cols.rearrange("p (m d f) -> p m d f", m=2, d=DT)

        def loads_of(b, c):
            half = c // 2
            return b * (16 * NCH // 2) + half * 16 + 16

        x_tiles = x.rearrange("(g j p) d -> g p j d", p=P, j=4)
        out_tiles = out.rearrange("(g j p) d -> g p j d", p=P, j=4)
        res_tiles = res.rearrange("(g j p) d -> g p j d", p=P, j=4)

        block = ctx.enter_context(nc.Block())

        @block.sync
        def _(sp):
            sp.dma_start(idst[:, :], ids).then_inc(ids_in, 16)
            for g in range(4):
                sp.dma_start(big[:, 4 * g:4 * g + 4, :], x_tiles[g]).then_inc(x_in[g], 16)
            for e in range(2):
                sp.dma_start(stream[:, e, :], wexp[:, e, :]).then_inc(exp_in[e], 16)
            sp.dma_start(lns[:, :, :], ln).then_inc(small_in, 16)
            sp.dma_start(gt[:, :], gates.broadcast_to([P, 2])).then_inc(small_in, 16)
            sp.dma_start(araw[:, :, :], amat).then_inc(small_in, 16)
            sp.dma_start(wstage[:, :, :], wov).then_inc(wov_in, 16)
            for e in range(2, E):
                sp.wait_ge(exp_hi, e - 1)
                sp.wait_ge(exp_lo, e - 1)
                sp.dma_start(stream[:, e % 2, :], wexp[:, e, :]).then_inc(exp_in[e % 2], 16)
            sp.wait_ge(zero_ok, 1)
            sp.dma_start(xs[T:T + P, :], ysb[:, :]).then_inc(tail_ok, 16)
            sp.wait_ge(tail_ok, 16)
            sp.wait_ge(scattered, 16 * NT)
            sp.wait_ge(bst_ok, 1)
            for k in range(3):
                sp.dma_start(braw[32 * k:32 * k + R, :], bmat).then_inc(b_in, 16)

            def item_rows(i):
                sp.wait_ge(items_ok, 1)
                return sp.value_load(itab[0:1, 0, bass.ds(i, 1)], min_val=0, max_val=T)

            def load_item(i):
                sp.dma_start(xi[:, :], xs[bass.ds(item_rows(i), P), :]).then_inc(xi_in, 16)

            def store_item(i):
                rows = item_rows(i)
                sp.wait_ge(y_copied, i + 1)
                sp.dma_start(ys[bass.ds(rows, P), :], ysb[:, :]).then_inc(y_stored, 16)

            sp.wait_ge(items_ok, 1)
            sp.wait_ge(scattered, 16 * NT)
            load_item(0)
            for i in range(1, 3):
                sp.wait_ge(x_turned, i)
                load_item(i)
            with sp.Fori(3, ITEMS) as i:
                sp.wait_ge(x_turned, i)
                load_item(i)
                store_item(i - 3)
            sp.wait_ge(vw_mm, 2)
            sp.dma_start(wstage[:, :, :], wqk).then_inc(wqk_in, 16)
            sp.dma_start(x1, x_tiles[0]).then_inc(x1_in, 16)
            for i in range(ITEMS - 3, ITEMS):
                store_item(i)

            def load_chunk(b, c, par, first=False):
                if not first:
                    sp.wait_ge(cg_lo, b * NCH + c - 1)
                sp.dma_start(stream[:, par, 0:CW], wmlp[:, bass.ds(c, 1), 0:CW]).then_inc(cg_in[par], 16)
                if not first:
                    sp.wait_ge(cd_lo, b * NCH + c - 1)
                sp.dma_start(stream[:, par, CW:CW + D], wmlp[:, bass.ds(c, 1), CW:CW + D]).then_inc(cd_in[par], 16)

            def load_stack(b, q, j):
                g = b * NQ + q
                if j == 0:
                    sp.wait_ge(qk_lo, g * 2 + 2)
                elif type(q) is int and j == 1:
                    pass
                else:
                    sp.wait_ge(s_done, g * (3 * QH) + (j - 1) * 3)
                rows = slice(HD * j, HD * j + HD)
                for k, (a, c) in enumerate(((Q_HI, K_HI), (Q_LO, K_HI), (Q_HI, K_LO))):
                    sp.dma_start(stack[HD * k:HD * k + HD, j % 2, :, :].bitcast(F32),
                                 qk[rows, a:c + 1:c - a, :].bitcast(F32)).then_inc(stk[j % 2], 16)

            def load_x(b):
                rows = x_tiles[bass.ds(b, 1)]
                sp.wait_ge(p_turned, b * (H * 3))
                sp.dma_start(x1, rows).then_inc(x1_in, 16)

            def store_residual(b):
                rows = res_tiles[bass.ds(b, 1)]
                sp.wait_ge(ln_own, (b + 1) * K_LN)
                sp.dma_start(rows, x1).then_inc(res_out, 16)
                sp.wait_ge(res_out, (b + 1) * 16)

            def load_residual(b, first=False):
                rows = res_tiles[bass.ds(b, 1)]
                if not first:
                    sp.wait_ge(out_in, b * 16)
                sp.dma_start(xt, rows).then_inc(res_in, 16)

            def batch(b, more):
                for c in range(2):
                    load_chunk(b, c, c, first=True)
                for j in range(QH):
                    load_stack(b, 0, j)
                with sp.Fori(1, NQ) as q:
                    for j in range(QH):
                        load_stack(b, q, j)
                if more:
                    load_x(b + 1)
                with sp.Fori(1, NCH // 2) as c2:
                    for par in range(2):
                        load_chunk(b, c2 * 2 + par, par)
                if more:
                    store_residual(b + 1)
                rows = out_tiles[bass.ds(b, 1)]
                sp.wait_ge(fin_out, b + 2)
                sp.dma_start(rows, xt).then_inc(out_in, 16)
                if more:
                    load_residual(b + 1)

            sp.wait_ge(exp_lo, E)
            store_residual(0)
            load_residual(0, first=True)
            with sp.Fori(0, NB - 1) as b:
                batch(b, True)
            batch(NB - 1, False)
            sp.wait_ge(out_in, NB * 16)
            sp.wait_ge(y_stored, ITEMS * 16)

        @block.gpsimd
        def _(pool):
            g = nc.gpsimd
            g.memset(ysb[:, :], 0.0).then_inc(zero_ok, 1)
            g.memset(ident[:, :], 0.0).then_inc(pool_own, 1)
            g.memset(ones[:, :], 1.0).then_inc(pool_own, 1)
            g.memset(act_sb[:, :], 0.0).then_inc(pool_own, 1)
            g.memset(zeror[:, :].bitcast(F32), 0.0).then_inc(pool_own, 1)
            g.memset(apad[:, :, :].bitcast(F32), 0.0).then_inc(pool_own, 1)
            g.iota(itab[:, 0, :], [[1, 20]], base=0, channel_multiplier=0).then_inc(pool_own, 1)
            pool.wait_ge(pool_own, 6)
            g.affine_select(out=ident[:, :], in_=ident[:, :], compare_op=ALU.not_equal, fill=1.0,
                            base=0, pattern=[[-1, P]], channel_multiplier=1).then_inc(const_ok, 1)
            g.affine_select(out=tri[:, :], in_=ones[:, :], compare_op=ALU.is_gt, fill=0.0,
                            base=0, pattern=[[1, P]], channel_multiplier=-1).then_inc(const_ok, 1)
            g.affine_select(out=act_sb[:, 0:P], in_=act_sb[:, 0:P], compare_op=ALU.is_ge, fill=MASKED,
                            base=0, pattern=[[-1, P]], channel_multiplier=1).then_inc(const_ok, 1)
            g.tensor_copy(itf[:, :], itab[:, 0, :]).then_inc(const_ok, 1)
            pool.wait_ge(const_ok, 4)
            g.tensor_copy(identr[:, :], ident[:, :]).then_inc(const_ok, 1)
            g.tensor_copy(maskr[:, :], act_sb[:, 0:P]).then_inc(const_ok, 1)
            pool.wait_ge(pos_ok, 1)
            for t in range(NT):
                pool.wait_ge(xn_ok, t + 1)
                g.indirect_dma_start(xs[0:T, :], bass.IndirectOffsetOnAxis(ap=pos[:, t:t + 1], axis=0),
                                     big[:, t, :], None).then_inc(scattered, 16)
            pool.wait_ge(scattered, 16 * NT)
            g.memset(braw, 0.0).then_inc(bst_ok, 1)
            pool.wait_ge(small_in, 48)
            for dt in range(DT):
                ins = g.tensor_scalar(asc[:, dt, :], araw[:, dt, :], lns[:, 1, dt:dt + 1], None, ALU.mult)
            ins.then_inc(pool_own, 1)
            pool.wait_ge(pool_own, 7)
            g.tensor_copy(apad[:, :, 0:R], asc[:, :, :]).then_inc(pool_own, 1)
            pool.wait_ge(pool_own, 8)
            g.tensor_tensor(apad[:, :, 32:32 + R], asc[:, :, :], apad[:, :, 0:R].bitcast(F32),
                            ALU.subtract).then_inc(apad_ok, 1)
            pool.wait_ge(b_in, 48)
            g.tensor_copy(bst[:, :], braw).then_inc(pool_own, 1)
            pool.wait_ge(pool_own, 9)
            g.tensor_tensor(bst[64:96, :], braw[64:96, :], bst[64:96, :].bitcast(F32),
                            ALU.subtract).then_inc(bst_ok, 1)

            pool.wait_ge(bst_ok, 2)
            pool.wait_ge(y_stored, 16 * ITEMS)
            for t in range(NT):
                if t and t % TT == 0:
                    pool.wait_ge(hb_turned, t)
                g.indirect_dma_start(hb[:, t % TT, :], None, ys[0:T, :],
                                     bass.IndirectOffsetOnAxis(ap=pos[:, t:t + 1], axis=0)).then_inc(y_in, 16)

        @block.tensor
        def _(pe):
            def split_product(dst, lhs, rhs, tiles, start=True, stop=True, skip=False):
                n = len(PARTS) * tiles
                i = 0
                for k in range(tiles):
                    for pl, pr in PARTS:
                        mm = pe.matmul(dst, lhs(pl, k), rhs(pr, k), start=start and i == 0,
                                       stop=stop and i == n - 1, skip_group_check=skip)
                        i += 1
                return mm

            pe.wait_ge(const_ok, 6)
            pe.wait_ge(onehot_ok, 1)
            ohf = oh[:, :, :].rearrange("p e t -> p (e t)")
            pe.matmul(bank[0][:, 0:64], tri[:, :], ohf, start=True, stop=True)
            pe.matmul(bank[0][:, 64:128], ones[:, :], ohf, start=True, stop=True).then_inc(ranks_ok, 1)

            pe.wait_ge(wov_in, 16)
            pe.wait_ge(small_in, 48)
            for ct in range(DT):
                for dt in range(DT):
                    mm = pe.matmul(bank[1][:, ct * R:ct * R + R],
                                   wstage[:, 0, dt * D + ct * P:dt * D + ct * P + P], araw[:, dt, :],
                                   start=dt == 0, stop=dt == DT - 1)
            mm.then_inc(woa_ok, 1)
            pe.wait_ge(bd_ok, 1)
            for dt in range(DT):
                for ct in range(DT):
                    mm = pe.matmul(bank[2 + dt // 2][:, 256 * (dt % 2) + 64 * ct:256 * (dt % 2) + 64 * ct + 64],
                                   wstage[:, 1, ct * D + dt * P:ct * D + dt * P + P],
                                   bd[:, ct, :, :].rearrange("p h r -> p (h r)"), start=True, stop=True)
                if dt % 2:
                    mm.then_inc(vw_mm, 1)

            XB, HB, AB, YB = 4, 5, 6, 7
            wflat = wr

            def turn_x(i, first=False):
                pe.wait_ge(xi_in, i * 16 + 16)
                if not first:
                    pe.wait_ge(xt_lo, i)
                for k in range(DT):
                    mm = pe.transpose(bank[XB][:, k * P:k * P + P], xi[:, k * P:k * P + P], ident[:, :])
                mm.then_inc(x_turned, 1)

            def first_product(w, i, first=False):
                pe.wait_ge(xt_lo, i + 1)
                if not first:
                    pe.wait_ge(h_gated, i)
                split_product(bank[HB][:, :], lambda p, k: xTs[:, p, k * P:k * P + P],
                              lambda p, k: wflat[:, p, bass.ds(w + k * D, D)], DT).then_inc(h_done, 1)

            def turn_act(i, first=False):
                pe.wait_ge(h_gated, i + 1)
                if not first:
                    pe.wait_ge(at_lo, i)
                for k in range(DT):
                    mm = pe.transpose(bank[AB][:, k * P:k * P + P], act_sb[:, k * P:k * P + P], ident[:, :])
                mm.then_inc(a_turned, 1)

            def second_product(w, i, first=False):
                pe.wait_ge(at_lo, i + 1)
                if not first:
                    pe.wait_ge(y_copied, i)
                split_product(bank[YB][:, :], lambda p, k: aTs[:, p, k * P:k * P + P],
                              lambda p, k: wflat[:, p, bass.ds(w + k * D, D)], DT).then_inc(y_done, 1)

            def weight_of(i):
                return pe.value_load(itab[0:1, 1, bass.ds(i, 1)], min_val=0, max_val=(E - 1) * EW)

            pe.wait_ge(items_ok, 1)
            pe.wait_ge(exp_hi, E)
            pe.wait_ge(exp_lo, E)
            turn_x(0, first=True)
            first_product(weight_of(0), 0, first=True)
            turn_x(1)
            turn_act(0, first=True)
            first_product(weight_of(1), 1)
            turn_x(2)
            second_product(weight_of(0), 0, first=True)
            turn_act(1)
            with pe.Fori(2, ITEMS - 1) as i:
                first_product(weight_of(i), i)
                turn_x(i + 1)
                second_product(weight_of(i - 1), i - 1)
                turn_act(i)
            last = ITEMS - 1
            first_product(weight_of(last), last)
            second_product(weight_of(last - 1), last - 1)
            turn_act(last)
            second_product(weight_of(last), last)

            pe.wait_ge(prep_ok, 1)
            pe.wait_ge(apad_ok, 1)

            def turn_rows(b, tiles):
                pe.wait_ge(hb_ok, b * TT + TT)
                for dt in tiles:
                    for tt in range(TT):
                        mm = pe.transpose(bank[ROWS[dt]][:, tt * P:tt * P + P], hb[:, tt, dt * P:dt * P + P],
                                          ident[:, :])
                    mm.then_inc(hb_turned, 1)

            def project(b, q, which):
                n = b * NQ + q
                pe.wait_ge(wq_hi, n + 1)
                pe.wait_ge(wq_lo, n + 1)
                if which:
                    pe.wait_ge(qk_lo, n * 2 + 1)
                split_product(bank[QKB][:, :], lambda p, k: wqs[:, p, which, k, :],
                              lambda p, k: hT[:, p, k, :], DT).then_inc(qk_done, 1)

            def scores(n, par, loads, first=False):
                pe.wait_ge(stk[par], loads)
                if not first:
                    pe.wait_ge(exp_ok, n * 4)
                for i, qt in enumerate((3, 2, 0, 1)):
                    bk, col, _ = SCORE[qt]
                    w = P * (qt + 1)
                    pe.matmul(bank[bk][:, col:col + w], stack[:, par, 0, qt * P:qt * P + P],
                              stack[:, par, 1, 0:w], start=True, stop=False, skip_group_check=True)
                    mm = pe.matmul(bank[bk][:, col + w - P:col + w], identr[:, :], maskr[:, :],
                                   start=False, stop=True, skip_group_check=True)
                    if qt != 2:
                        mm.then_inc(s_done, 1)

            def turn_probs(n, par, first=False):
                pe.wait_ge(pn_ok, n * 4 + 4)
                for kt in (0, 1, 3, 2):
                    bk, col, _ = TURNED[kt]
                    if not first and kt != 3:
                        pe.wait_ge(pt_lo, (n - 1) * 3 + (1, 2, 3)[kt])
                    for qt in range(kt, TT):
                        src = SCORE[qt][2] + kt * P
                        mm = pe.transpose(bank[bk][:, col + (qt - kt) * P:col + (qt - kt) * P + P],
                                          prob[par][:, src:src + P], ident[:, :])
                    if kt != 1:
                        mm.then_inc(p_turned, 1)

            def attend(b, q, n, j):
                pe.wait_ge(pt_lo, n * 3 + 3)
                pe.wait_ge(vst_lo, b * NQ + q + 1)
                for kt in range(TT):
                    _, _, at = TURNED[kt]
                    w = S - kt * P
                    for part in (HI, LO):
                        mm = pe.matmul(bank[ATT][:, kt * P:S], vst[:, kt, 64 * j:64 * j + P],
                                       pts[:, j % 2, part, at:at + w], start=False, stop=False, skip_group_check=True)
                mm.then_inc(pv_done, 1)

            def head_step(b, q, j, ahead):
                n = (b * NQ + q) * QH + j
                if ahead or j < QH - 2:
                    m = b * (H // 2) + q * 2 + (j + 2) // 2
                    scores(n + 2, j % 2, m * 48 + 48)
                if j == 0 and ahead:
                    project(b, q + 1, 1)
                if j == 3 and ahead == 2:
                    project(b, q + 2, 0)
                if ahead or j < QH - 1:
                    turn_probs(n + 1, (j + 1) % 2)
                attend(b, q, n, j)

            def gate_up(b, c, par, first=False):
                n = b * NCH + c
                pe.wait_ge(cg_hi, n + 1)
                pe.wait_ge(cg_lo, n + 1)
                if not first:
                    pe.wait_ge(gu_ok, n)
                split_product(bank[GATE][:, :], lambda p, k: wch[:, par, p, k * P:k * P + P],
                              lambda p, k: hT[:, p, k, :], DT, stop=False)
                pe.matmul(bank[GATE][:, :], bchunk[:, par, :], zst[:, :], start=False,
                          stop=True).then_inc(g_done, 1)
                split_product(bank[UP][:, :], lambda p, k: wch[:, par, p, (DT + k) * P:(DT + k) * P + P],
                              lambda p, k: hT[:, p, k, :], DT).then_inc(u_done, 1)

            def down(b, c, par):
                n = b * NCH + c
                pe.wait_ge(gu_lo, n + 1)
                pe.wait_ge(cd_lo, n + 1)
                for tt in range(TT):
                    mm = split_product(bank[Y0 + tt][:, :], lambda p, k: actr[:, par, p, tt * P:tt * P + P],
                                       lambda p, k: wch[:, par, p, CW:CW + D], 1, start=False, stop=False, skip=True)
                mm.then_inc(d_done, 1)

            def batch(b, more):
                pe.wait_ge(ht_lo, b * 4 + 4)
                for tt in range(TT):
                    mm = split_product(bank[VALUES[tt // 2]][:, 256 * (tt % 2):256 * (tt % 2) + 256],
                                       lambda p, k: hT[:, p, k, tt * P:tt * P + P],
                                       lambda p, k: vw[:, p, k, :], DT)
                    if tt % 2:
                        mm.then_inc(vp_done, 1)
                for k in range(DT):
                    for part in (HI, LO):
                        mm = pe.matmul(bank[LOW_RANK][:, :], apad[:, k, :], hT[:, part, k, :],
                                       start=k == 0 and part == HI, stop=k == DT - 1 and part == LO)
                mm.then_inc(ha_done, 1)
                pe.wait_ge(fin_out, b + 1)
                for which in range(2):
                    project(b, 0, which)
                pe.wait_ge(vp_copied, b * 2 + 2)
                pe.wait_ge(ha_ok, b + 1)
                pe.matmul(bank[ATT][:, :], zeror[:, :], hT[:, HI, 0, :], start=True, stop=False,
                          skip_group_check=True).then_inc(pv_done, 1)
                scores(b * H, 0, b * (H // 2) * 48 + 48, first=True)
                scores(b * H + 1, 1, b * (H // 2) * 48 + 48)
                project(b, 1, 0)
                turn_probs(b * H, 0, first=True)
                with pe.Fori(0, NQ - 2) as q:
                    for j in range(QH):
                        head_step(b, q, j, 2)
                for q, ahead in ((NQ - 2, 1), (NQ - 1, 0)):
                    for j in range(QH):
                        head_step(b, q, j, ahead)
                pe.wait_ge(exp_ok, (b + 1) * H * 4)
                pe.wait_ge(zs_ok, b + 1)
                for tt in range(TT):
                    pe.matmul(bank[Y0 + tt][:, :], zeror[:, :], hT[:, HI, 0, :], start=True, stop=False,
                              skip_group_check=True)
                gate_up(b, 0, 0, first=True)
                with pe.Fori(0, NCH // 2 - 1) as c2:
                    gate_up(b, c2 * 2 + 1, 1)
                    down(b, c2 * 2, 0)
                    gate_up(b, c2 * 2 + 2, 0)
                    down(b, c2 * 2 + 1, 1)
                gate_up(b, NCH - 1, 1)
                if more:
                    turn_rows(b + 1, (0, 1))
                down(b, NCH - 2, 0)
                if more:
                    pe.wait_ge(gu_ok, (b + 1) * NCH)
                    turn_rows(b + 1, (2, 3))
                down(b, NCH - 1, 1)

            turn_rows(0, range(DT))
            with pe.Fori(0, NB - 1) as b:
                batch(b, True)
            batch(NB - 1, False)

        @block.scalar
        def _(act):
            a = nc.scalar

            def copy(dst, src):
                return a.activation(dst, src, ACT.Copy)

            act.wait_ge(small_in, 48)
            a.activation(tg[:, :], gt[:, :], ACT.Tanh).then_inc(tanh_ok, 1)
            def expert_high(e):
                act.wait_ge(exp_in[e % 2], 16 * (e // 2 + 1))
                copy(wr[:, HI, e * EW:(e + 1) * EW], stream[:, e % 2, :]).then_inc(exp_hi, 1)

            for half in range(2):
                for t in range(NT // 2 * half, NT // 2 * (half + 1)):
                    act.wait_ge(norm_ok, half + 1)
                    a.activation(big[:, t, :], big[:, t, :], ACT.Identity, bias=lnb[:, t:t + 1],
                                 scale=lna[:, t:t + 1]).then_inc(xn_ok, 1)
                if half == 0:
                    expert_high(0)
                    expert_high(1)
            expert_high(2)
            expert_high(3)
            act.wait_ge(vw_mm, 2)
            for dt in range(DT):
                a.activation(vw[:, HI, dt, :], bank[2 + dt // 2][:, 256 * (dt % 2):256 * (dt % 2) + 256],
                             ACT.Copy, scale=lns[:, 0, dt:dt + 1]).then_inc(vw_hi, 1)

            def x_high(i, first=False):
                act.wait_ge(x_turned, i + 1)
                if not first:
                    act.wait_ge(h_done, i)
                copy(xTs[:, HI, :], bank[4][:, :]).then_inc(xt_hi, 1)

            def silu(i, first=False):
                act.wait_ge(h_done, i + 1)
                if not first:
                    act.wait_ge(h_gated, i)
                a.activation(sil[:, :], bank[5][:, :], ACT.Silu).then_inc(h_silu, 1)

            def act_high(i, first=False):
                act.wait_ge(a_turned, i + 1)
                if not first:
                    act.wait_ge(y_done, i)
                copy(aTs[:, HI, :], bank[6][:, :]).then_inc(at_hi, 1)

            def copy_y(i, first=False):
                act.wait_ge(y_done, i + 1)
                if first:
                    act.wait_ge(tail_ok, 16)
                else:
                    act.wait_ge(y_stored, i * 16)
                copy(ysb[:, :], bank[7][:, :]).then_inc(y_copied, 1)

            x_high(0, first=True)
            silu(0, first=True)
            x_high(1)
            act_high(0, first=True)
            silu(1)
            x_high(2)
            copy_y(0, first=True)
            act_high(1)
            with act.Fori(2, ITEMS - 1) as i:
                silu(i)
                x_high(i + 1)
                copy_y(i - 1)
                act_high(i)
            last = ITEMS - 1
            silu(last)
            copy_y(last - 1)
            act_high(last)
            copy_y(last)

            def split_wqk(b, q):
                copy(wqs[:, HI, :, :, :], wqk_v[:, :, :, bass.ds(q * P, P)]).then_inc(wq_hi, 1)

            def split_qk(b, q, which, first=False):
                n = b * NQ + q
                act.wait_ge(qk_done, n * 2 + which + 1)
                if which == 0 and not first:
                    for k in range(2):
                        act.wait_ge(stk[k], n * 96)
                copy(qk[:, (Q_HI, K_HI)[which], :], bank[QKB][:, :]).then_inc(qk_hi, 1)

            def exponentials(n, par):
                for qt, maxima in ((3, 1), (2, 3), (0, 3), (1, 4)):
                    act.wait_ge(nb_ok, n * 4 + maxima)
                    bk, col, at = SCORE[qt]
                    w = P * (qt + 1)
                    a.activation(prob[par][:, at:at + w], bank[bk][:, col:col + w], ACT.Exp,
                                 bias=nb[:, qt:qt + 1], accum_out=rs[:, par, qt:qt + 1]).then_inc(exp_ok, 1)

            def head_step(b, q, j, one_more=True):
                n = (b * NQ + q) * QH + j
                if one_more:
                    exponentials(n + 1, (j + 1) % 2)
                if j == 0:
                    act.wait_ge(pv_done, b + 1 + n)
                    act.wait_ge(vp_copied, b * 2 + 2)
                    act.wait_ge(vst_zero, 1)
                    copy(vst_v[:, :, :, 0:R], vp[:, :, bass.ds(q * QH, QH), :]).then_inc(vst_hi, 1)
                for i, (bk, w, at) in enumerate(((4, 512, 0), (5, 512, 512), (6, 256, 1024))):
                    act.wait_ge(p_turned, n * 3 + i + 1)
                    copy(pts[:, j % 2, HI, at:at + w], bank[bk][:, 0:w]).then_inc(pt_hi, 1)

            def quad(b, q, ahead):
                for j in range(QH):
                    head_step(b, q, j, ahead or j < QH - 1)
                    if j == 0 and ahead:
                        split_qk(b, q + 1, 1)
                    if j == 1 and ahead == 2:
                        split_wqk(b, q + 2)
                    if j == 3 and ahead == 2:
                        split_qk(b, q + 2, 0)

            def split_gate_up(b, c, par):
                act.wait_ge(cg_in[par], loads_of(b, c))
                raw, dst = gu_view(stream[:, par, 0:CW]), gu_view(wch[:, par, HI, 0:CW])
                for dt in range(DT):
                    ins = a.activation(dst[:, :, dt, :], raw[:, :, dt, :], ACT.Copy, scale=lns[:, 1, dt:dt + 1])
                ins.then_inc(cg_hi, 1)

            def chunk_step(b, c, par, more=True):
                n = b * NCH + c
                act.wait_ge(g_done, n + 1)
                a.activation(sil[:, :], bank[GATE][:, :], ACT.Silu).then_inc(g_silu, 1)
                act.wait_ge(cd_in[par], loads_of(b, c))
                copy(wch[:, par, HI, CW:CW + D], stream[:, par, CW:CW + D]).then_inc(cd_hi, 1)
                act.wait_ge(gu_ok, n + 1)
                copy(actr[:, par, HI, :], act_sb[:, :]).then_inc(gu_hi, 1)
                if more:
                    split_gate_up(b, c + 2, par)

            def norm_rows(b, j):
                act.wait_ge(ln_ok, b + 1)
                a.activation(hbf[:, bass.ds(j * D, D)], x1f[:, bass.ds(j * D, D)], ACT.Identity,
                             bias=lnb[:, bass.ds(j, 1)], scale=lna[:, bass.ds(j, 1)]).then_inc(hb_ok, 1)

            def rows_high(b):
                for dt in range(DT):
                    act.wait_ge(hb_turned, b * 4 + dt + 1)
                    copy(hT[:, HI, dt, :], bank[ROWS[dt]][:, :]).then_inc(ht_hi, 1)

            def batch(b, more):
                for k in range(2):
                    act.wait_ge(vp_done, b * 2 + k + 1)
                    copy(vp[:, 2 * k:2 * k + 2, :, :].rearrange("p t h r -> p (t h r)"),
                         bank[VALUES[k]][:, :]).then_inc(vp_copied, 1)
                act.wait_ge(ha_done, b + 1)
                copy(att_low, bank[LOW_RANK][32:32 + R, :]).then_inc(ha_low, 1)
                for which in range(2):
                    split_qk(b, 0, which, first=True)
                split_wqk(b, 1)
                act.wait_ge(res_out, (b + 1) * 16)
                exponentials(b * H, 0)
                split_qk(b, 1, 0)
                with act.Fori(0, NQ - 2) as q:
                    quad(b, q, 2)
                quad(b, NQ - 2, 1)
                quad(b, NQ - 1, 0)
                for par in range(2):
                    split_gate_up(b, par, par)
                act.wait_ge(pv_done, (b + 1) * (H + 1))
                copy(att_low, bank[ATT][32:32 + R, :]).then_inc(at_low, 1)
                act.wait_ge(at_sum, b + 1)
                a.activation(att_low, att_sum, ACT.Tanh).then_inc(mod_ok, 1)
                act.wait_ge(z_ok, b + 1)
                copy(zst[0:R, :], zrow)
                copy(zst[64:64 + R, :], zrow).then_inc(zs_hi, 1)
                if more:
                    with act.Fori(0, NORM_AT) as c2:
                        for par in range(2):
                            chunk_step(b, c2 * 2 + par, par)
                    with act.Fori(NORM_AT, NORM_AT + 2) as c2:
                        for par in range(2):
                            chunk_step(b, c2 * 2 + par, par)
                            norm_rows(b + 1, c2 * 2 + par - 2 * NORM_AT)
                    with act.Fori(NORM_AT + 2, NCH // 2 - 1) as c2:
                        for par in range(2):
                            chunk_step(b, c2 * 2 + par, par)
                    split_wqk(b + 1, 0)
                else:
                    with act.Fori(0, NCH // 2 - 1) as c2:
                        for par in range(2):
                            chunk_step(b, c2 * 2 + par, par)
                chunk_step(b, NCH - 2, 0, more=False)
                chunk_step(b, NCH - 1, 1, more=False)
                if more:
                    rows_high(b + 1)

            for j in range(TT):
                norm_rows(0, j)
            rows_high(0)
            act.wait_ge(wqk_ok, 1)
            split_wqk(0, 0)
            act.wait_ge(bst_ok, 2)
            with act.Fori(0, NB - 1) as b:
                batch(b, True)
            batch(NB - 1, False)

        @block.vector
        def _(dve):
            v = nc.vector
            own = [0]

            def step(ins):
                own[0] += 1
                return ins.then_inc(dve_own, 1)

            def settle():
                dve.wait_ge(dve_own, own[0])

            def link(ins):
                step(ins)
                settle()

            step(v.memset(ge[:, 0, :], 1.0))
            step(v.memset(ge[:, E, :], 0.0))
            step(v.memset(small[:, :, :], 0.0))
            dve.wait_ge(ids_in, 16)
            link(v.tensor_copy(idf[:, :], idst[:, :]))
            for e in range(1, E):
                step(v.tensor_scalar(ge[:, e, :], idf[:, :], float(e * PER_EXPERT), None, ALU.is_ge))
            settle()
            v.tensor_tensor(oh[:, :, :], ge[:, 0:E, :], ge[:, 1:E + 1, :], ALU.subtract).then_inc(onehot_ok, 1)
            dve.wait_ge(ranks_ok, 1)
            dve.wait_ge(onehot_ok, 1)
            link(v.tensor_copy(cnt[:, :, :].rearrange("p a b -> p (a b)"), bank[0][:, 0:2 * E * NT]))
            total = cnt[:, 1, :]
            dve.wait_ge(const_ok, 6)
            link(v.tensor_tensor_scan(cum[:, :], ones[:, 0:E * NT], total, 0.0, ALU.mult, ALU.add))
            link(v.tensor_tensor(exc[:, :], cum[:, :], total, ALU.subtract))
            pef = pe_[:, :, :].rearrange("p e t -> p (e t)")
            link(v.tensor_tensor(pef, exc[:, :], cnt[:, 0, :], ALU.add))
            link(v.tensor_tensor(pef, pef, oh[:, :, :].rearrange("p e t -> p (e t)"), ALU.mult))
            link(v.tensor_reduce(posf[:, :], pe_[:, :, :].rearrange("p e t -> p t e"), AXX, ALU.add))
            v.tensor_copy(pos[:, :], posf[:, :]).then_inc(pos_ok, 1)
            def slot(k, width=8, start=0):
                return nr[:, 8 * k + start:8 * k + start + width]

            def aggregate(n, mark, done):
                done()
                mark(v.memset(slot(CARRIER), 0.0))
                for j in range(n):
                    mark(v.bn_aggr(mv[:, j, :], st[:, 6 * j:6 * j + 6]))
                done()

            def root_guess(mark, done):
                mark(v.tensor_scalar(nri[:, :], slot(ARG).bitcast(I32), 1, None, ALU.arith_shift_right))
                done()
                mark(v.tensor_scalar(slot(ROOT).bitcast(I32), nri[:, :], -1.0, float(0x5F3759DF), ALU.mult, ALU.add))
                done()

            def root_step(mark, done):
                mark(v.tensor_tensor(slot(TA), slot(ROOT), slot(ROOT), ALU.mult))
                done()
                mark(v.tensor_tensor(slot(TB), slot(TA), slot(ARG), ALU.mult))
                done()
                mark(v.tensor_scalar(slot(TA), slot(TB), -0.5, 1.5, ALU.mult, ALU.add))
                done()
                mark(v.tensor_tensor(slot(ROOT), slot(ROOT), slot(TA), ALU.mult))
                done()

            ARG, ROOT, TA, TB, SM, T1, T2, CARRIER = range(8)
            for half in range(2):
                for j in range(8):
                    if j % 4 == 0:
                        dve.wait_ge(x_in[2 * half + j // 4], 16)
                    step(v.bn_stats(st[:, 6 * j:6 * j + 6], big[:, 8 * half + j, :]))
                aggregate(8, step, settle)
                link(v.tensor_scalar(slot(ARG), mv[:, :, 1], LN_EPS, None, ALU.add))
                root_guess(step, settle)
                for _ in range(3):
                    root_step(step, settle)
                link(v.scalar_tensor_tensor(out=lnb[:, 8 * half:8 * half + 8], in0=mv[:, :, 0], scalar=-1.0,
                                            in1=slot(ROOT), op0=ALU.mult, op1=ALU.mult))
                v.tensor_copy(lna[:, 8 * half:8 * half + 8], slot(ROOT)).then_inc(norm_ok, 1)

            def expert_low(e):
                dve.wait_ge(exp_hi, e + 1)
                v.tensor_tensor(wr[:, LO, e * EW:(e + 1) * EW], stream[:, e % 2, :],
                                wr[:, HI, e * EW:(e + 1) * EW].bitcast(F32), ALU.subtract).then_inc(exp_lo, 1)

            expert_low(0)
            expert_low(1)
            OFF, CNT, NTF, TIN, TEX, DD, DIF = range(7)
            off, excv, cumv = small[:, OFF, :], exc[:, :].rearrange("p (e t) -> p e t", e=E), cum[:, :].rearrange("p (e t) -> p e t", e=E)
            link(v.tensor_copy(off, excv[:, :, 0]))
            link(v.tensor_tensor(small[:, CNT, :], cumv[:, :, NT - 1], off, ALU.subtract))
            link(v.tensor_scalar(nti[:, :], small[:, CNT, :], float(P - 1), None, ALU.add))
            link(v.tensor_scalar(nti[:, :], nti[:, :], P.bit_length() - 1, None, ALU.logical_shift_right))
            link(v.tensor_copy(small[:, NTF, :], nti[:, :]))
            link(v.tensor_tensor_scan(small[:, TIN, :], ones[:, 0:E], small[:, NTF, :], 0.0, ALU.mult, ALU.add))
            link(v.tensor_tensor(small[:, TEX, :], small[:, TIN, :], small[:, NTF, :], ALU.subtract))
            link(v.scalar_tensor_tensor(out=small[:, DD, :], in0=small[:, TEX, :], scalar=-float(P), in1=off,
                                        op0=ALU.mult, op1=ALU.add))
            link(v.tensor_tensor(small[:, DIF, 1:E], small[:, DD, 1:E], small[:, DD, 0:E - 1], ALU.subtract))
            step(v.tensor_scalar(its[:, 0, :], itf[:, :], float(P), None, ALU.mult))
            step(v.memset(its[:, 1, :], 0.0))
            settle()
            for e in range(1, E):
                edge = small[:, TEX, e:e + 1]
                step(v.tensor_scalar(its[:, 2, :], itf[:, :], edge, small[:, DIF, e:e + 1], ALU.is_ge, ALU.mult))
                link(v.scalar_tensor_tensor(out=its[:, 1, :], in0=itf[:, :], scalar=edge, in1=its[:, 1, :],
                                            op0=ALU.is_ge, op1=ALU.add))
                link(v.tensor_tensor(its[:, 0, :], its[:, 0, :], its[:, 2, :], ALU.add))
            step(v.tensor_scalar(itab[:, 0, :], its[:, 0, :], float(T), None, ALU.min))
            step(v.tensor_scalar(itab[:, 1, :], its[:, 1, :], float(EW), None, ALU.mult))
            dve.wait_ge(dve_own, own[0])
            v.tensor_copy(small[:, 15, :], small[:, DD, :]).then_inc(items_ok, 1)

            link(v.memset(bd[:, :, :, :], 0.0))
            dve.wait_ge(woa_ok, 1)
            woa = bank[1][:, 0:DT * R].rearrange("p (c r) -> p c r", c=DT)
            for h in range(QH):
                rows = slice(HD * h, HD * h + HD)
                ins = v.tensor_copy(bd[rows, :, h, :], woa[rows, :, :])
            ins.then_inc(bd_ok, 1)
            expert_low(2)
            expert_low(3)
            dve.wait_ge(vw_hi, DT)
            for dt in range(DT):
                ins = v.scalar_tensor_tensor(
                    out=vw[:, LO, dt, :], in0=bank[2 + dt // 2][:, 256 * (dt % 2):256 * (dt % 2) + 256],
                    scalar=lns[:, 0, dt:dt + 1], in1=vw[:, HI, dt, :].bitcast(F32), op0=ALU.mult, op1=ALU.subtract)
            ins.then_inc(prep_ok, 1)

            def x_low(i):
                dve.wait_ge(xt_hi, i + 1)
                v.tensor_tensor(xTs[:, LO, :], bank[4][:, :], xTs[:, HI, :].bitcast(F32),
                                ALU.subtract).then_inc(xt_lo, 1)

            def gated(i):
                dve.wait_ge(h_silu, i + 1)
                v.tensor_tensor(act_sb[:, :], bank[5][:, :], sil[:, :], ALU.mult).then_inc(h_gated, 1)

            def act_low(i):
                dve.wait_ge(at_hi, i + 1)
                v.tensor_tensor(aTs[:, LO, :], bank[6][:, :], aTs[:, HI, :].bitcast(F32),
                                ALU.subtract).then_inc(at_lo, 1)

            x_low(0)
            gated(0)
            x_low(1)
            act_low(0)
            with dve.Fori(1, ITEMS - 1) as i:
                gated(i)
                x_low(i + 1)
                act_low(i)
            gated(ITEMS - 1)
            act_low(ITEMS - 1)

            dve.wait_ge(wqk_in, 16)
            for dt in range(DT):
                v.tensor_scalar(wqk_v[:, 0, dt, :], wqk_v[:, 0, dt, :], lns[:, 0, dt:dt + 1], SCALE, ALU.mult, ALU.mult)
                ins = v.tensor_scalar(wqk_v[:, 1, dt, :], wqk_v[:, 1, dt, :], lns[:, 0, dt:dt + 1], None, ALU.mult)
            ins.then_inc(wqk_ok, 1)
            dve.wait_ge(y_done, ITEMS)
            v.memset(vst.bitcast(F32), 0.0).then_inc(vst_zero, 1)
            v.memset(zst[:, :].bitcast(F32), 0.0).then_inc(vst_zero, 1)
            v.memset(slot(CARRIER), 0.0).then_inc(fin_out, 1)

            def low(dst, src, high, done):
                v.tensor_tensor(dst, src, high.bitcast(F32), ALU.subtract).then_inc(done, 1)

            def wqk_low(b, q):
                dve.wait_ge(wq_hi, b * NQ + q + 1)
                low(wqs[:, LO, :, :, :], wqk_v[:, :, :, bass.ds(q * P, P)], wqs[:, HI, :, :, :], wq_lo)

            def qk_low(b, q, which):
                dve.wait_ge(qk_hi, (b * NQ + q) * 2 + which + 1)
                low(qk[:, (Q_LO, K_LO)[which], :], bank[QKB][:, :], qk[:, (Q_HI, K_HI)[which], :], qk_lo)

            def maxima(n):
                for i, qts in enumerate(((3,), (2, 0), (1,))):
                    dve.wait_ge(s_done, n * 3 + i + 1)
                    for qt in qts:
                        bk, col, _ = SCORE[qt]
                        v.reduce_max(nb[:, qt:qt + 1], bank[bk][:, col:col + P * (qt + 1)], AXX,
                                     negate=True).then_inc(nb_ok, 1)

            def normalise(n, par):
                dve.wait_ge(exp_ok, n * 4 + 4)
                v.reciprocal(rr[:, :], rs[:, par, :]).then_inc(rr_ok, 1)
                dve.wait_ge(rr_ok, n + 1)
                for qt in (3, 2, 0, 1):
                    at = SCORE[qt][2]
                    rows = prob[par][:, at:at + P * (qt + 1)]
                    v.tensor_scalar(rows, rows, rr[:, qt:qt + 1], None, ALU.mult).then_inc(pn_ok, 1)

            def head_step(b, q, j, two_more=True, one_more=True):
                n = (b * NQ + q) * QH + j
                if one_more:
                    normalise(n + 1, (j + 1) % 2)
                if two_more:
                    maxima(n + 2)
                if j == 0:
                    dve.wait_ge(vst_hi, b * NQ + q + 1)
                    low(vst_v[:, :, :, 32:32 + R], vp[:, :, bass.ds(q * QH, QH), :], vst_v[:, :, :, 0:R], vst_lo)
                for i, (bk, w, at) in enumerate(((4, 512, 0), (5, 512, 512), (6, 256, 1024))):
                    dve.wait_ge(pt_hi, n * 3 + i + 1)
                    low(pts[:, j % 2, LO, at:at + w], bank[bk][:, 0:w], pts[:, j % 2, HI, at:at + w], pt_lo)

            def quad(b, q, ahead):
                last = ahead == 0
                for j in range(QH):
                    head_step(b, q, j, not last or j < QH - 2, not last or j < QH - 1)
                    if j == 0 and ahead:
                        qk_low(b, q + 1, 1)
                    if j == 1 and ahead == 2:
                        wqk_low(b, q + 2)
                    if j == 3 and ahead == 2:
                        qk_low(b, q + 2, 0)

            def gate_up_low(b, c, par):
                dve.wait_ge(cg_hi, b * NCH + c + 1)
                raw, high, dst = (gu_view(t) for t in (stream[:, par, 0:CW], wch[:, par, HI, 0:CW], wch[:, par, LO, 0:CW]))
                for dt in range(DT):
                    ins = v.scalar_tensor_tensor(out=dst[:, :, dt, :], in0=raw[:, :, dt, :], scalar=lns[:, 1, dt:dt + 1],
                                                 in1=high[:, :, dt, :].bitcast(F32), op0=ALU.mult, op1=ALU.subtract)
                v.tensor_copy(bchunk[:, par, :], bst[:, bass.ds(c * P, P)].bitcast(F32)).then_inc(cg_lo, 1)

            def down_low(b, c, par):
                dve.wait_ge(cd_hi, b * NCH + c + 1)
                low(wch[:, par, LO, CW:CW + D], stream[:, par, CW:CW + D], wch[:, par, HI, CW:CW + D], cd_lo)

            def chunk_step(b, c, par, more=True):
                n = b * NCH + c
                down_low(b, c, par)
                dve.wait_ge(g_silu, n + 1)
                dve.wait_ge(u_done, n + 1)
                v.tensor_tensor(act_sb[:, :], bank[UP][:, :], sil[:, :], ALU.mult).then_inc(gu_ok, 1)
                dve.wait_ge(gu_hi, n + 1)
                low(actr[:, par, LO, :], act_sb[:, :], actr[:, par, HI, :], gu_lo)
                dve.wait_ge(gu_lo, n + 1)
                if more:
                    gate_up_low(b, c + 2, par)

            def x1_tile(b, j):
                dve.wait_ge(x1_in, b * 16 + 16)
                dve.wait_ge(y_in, (b + 1) * 16 * TT)
                dve.wait_ge(tanh_ok, 1)
                rows = x1f[:, bass.ds(j * D, D)]
                v.scalar_tensor_tensor(out=rows, in0=hbf[:, bass.ds(j * D, D)], scalar=tg[:, 0:1], in1=rows,
                                       op0=ALU.mult, op1=ALU.add).then_inc(ln_own, 1)
                dve.wait_ge(ln_own, b * K_LN + j * 2 + 1)
                v.bn_stats(st[:, bass.ds(j * 6, 6)], rows).then_inc(ln_own, 1)

            def norm_factors(b, half):
                mine = [2 * TT if half == 0 else 2 * TT + 13]

                def mark(ins):
                    mine[0] += 1
                    ins.then_inc(ln_own, 1)

                def done():
                    dve.wait_ge(ln_own, b * K_LN + mine[0])

                mean, var = mv[:, 0:TT, 0], mv[:, 0:TT, 1]
                r1, r2 = slot(ROOT, TT), slot(ROOT, TT, TT)
                if half == 0:
                    aggregate(TT, mark, done)
                    mark(v.tensor_scalar(slot(ARG, TT), var, LN_EPS, None, ALU.add))
                    done()
                    mark(v.scalar_tensor_tensor(out=slot(ARG, TT, TT), in0=slot(ARG, TT), scalar=RMS_EPS, in1=var,
                                                op0=ALU.mult, op1=ALU.add))
                    done()
                    root_guess(mark, done)
                    root_step(mark, done)
                    assert mine[0] == 2 * TT + 13, mine[0]
                    return
                for _ in range(2):
                    root_step(mark, done)
                mark(v.scalar_tensor_tensor(out=lnb[:, 0:TT], in0=mean, scalar=-1.0, in1=r2,
                                            op0=ALU.mult, op1=ALU.mult))
                mark(v.tensor_scalar(slot(T1, TT), r1, tg[:, 1:2], None, ALU.mult))
                done()
                mark(v.scalar_tensor_tensor(out=slot(T2, TT), in0=mean, scalar=-1.0, in1=slot(T1, TT),
                                            op0=ALU.mult, op1=ALU.mult))
                mark(v.tensor_scalar(slot(SM, TT), slot(T1, TT), 1.0, None, ALU.add))
                done()
                v.tensor_copy(lna[:, 0:TT], r2).then_inc(ln_ok, 1)
                assert mine[0] == K_LN - TT, mine[0]

            def residual(b, j):
                rows = x1f[:, bass.ds(j * D, D)]
                factor, term = nr[:, bass.ds(j + 8 * SM, 1)], nr[:, bass.ds(j + 8 * T2, 1)]
                dve.wait_ge(hb_ok, b * TT + j + 1)
                v.tensor_scalar(rows, rows, factor, term, ALU.mult, ALU.add).then_inc(ln_own, 1)

            def rows_low(b):
                for dt in range(DT):
                    dve.wait_ge(ht_hi, b * 4 + dt + 1)
                    low(hT[:, LO, dt, :], bank[ROWS[dt]][:, :], hT[:, HI, dt, :], ht_lo)

            def batch(b, more):
                dve.wait_ge(ha_low, b + 1)
                v.tensor_tensor(haT, bank[LOW_RANK][0:R, :], att_low, ALU.add).then_inc(ha_ok, 1)
                for which in range(2):
                    qk_low(b, 0, which)
                maxima(b * H)
                wqk_low(b, 1)
                normalise(b * H, 0)
                maxima(b * H + 1)
                qk_low(b, 1, 0)
                with dve.Fori(0, NQ - 2) as q:
                    quad(b, q, 2)
                quad(b, NQ - 2, 1)
                quad(b, NQ - 1, 0)
                for par in range(2):
                    gate_up_low(b, par, par)
                dve.wait_ge(at_low, b + 1)
                v.tensor_tensor(att_sum, bank[ATT][0:R, :], att_low, ALU.add).then_inc(at_sum, 1)
                dve.wait_ge(mod_ok, b + 1)
                v.scalar_tensor_tensor(out=zrow, in0=att_low, scalar=MOD_SCALE, in1=haT,
                                       op0=ALU.mult, op1=ALU.mult).then_inc(z_ok, 1)
                dve.wait_ge(zs_hi, b + 1)
                low(zst[32:32 + R, :], zrow, zst[0:R, :], zs_ok)
                if more:
                    for par in range(2):
                        chunk_step(b, par, par)
                    with dve.Fori(1, 1 + TT // 2) as c2:
                        for par in range(2):
                            chunk_step(b, c2 * 2 + par, par)
                            x1_tile(b + 1, c2 * 2 + par - 2)
                    for par in range(2):
                        chunk_step(b, 2 + TT + par, par)
                        norm_factors(b + 1, par)
                    with dve.Fori(NORM_AT, NORM_AT + TT // 2) as c2:
                        for par in range(2):
                            chunk_step(b, c2 * 2 + par, par)
                            residual(b + 1, c2 * 2 + par - 2 * NORM_AT)
                    with dve.Fori(NORM_AT + TT // 2, NCH // 2 - 1) as c2:
                        for par in range(2):
                            chunk_step(b, c2 * 2 + par, par)
                    wqk_low(b + 1, 0)
                else:
                    with dve.Fori(0, NCH // 2 - 1) as c2:
                        for par in range(2):
                            chunk_step(b, c2 * 2 + par, par)
                chunk_step(b, NCH - 2, 0, more=False)
                chunk_step(b, NCH - 1, 1, more=False)
                if more:
                    rows_low(b + 1)
                dve.wait_ge(res_in, b * 16 + 16)
                dve.wait_ge(d_done, (b + 1) * NCH)
                for tt in range(TT):
                    ins = v.scalar_tensor_tensor(out=xt[:, tt, :], in0=bank[Y0 + tt][:, :], scalar=tg[:, 1:2],
                                                 in1=xt[:, tt, :], op0=ALU.mult, op1=ALU.add)
                ins.then_inc(fin_out, 1)

            for j in range(TT):
                x1_tile(0, j)
            norm_factors(0, 0)
            norm_factors(0, 1)
            for j in range(TT):
                residual(0, j)
            rows_low(0)
            wqk_low(0, 0)
            with dve.Fori(0, NB - 1) as b:
                batch(b, True)
            batch(NB - 1, False)


def kernel(x, itok_BxS_13_99985, ctx_2048, g_xattn, g_ffn, L0_ffn_ln1_w, L0_ffn_ln2_w, L0_ffn_Wq, L0_ffn_Wk,
           L0_ffn_Wv, L0_ffn_Wo, L0_ffn_A, L0_ffn_B, L0_ffn_W_in_base, L0_ffn_W_up_base, L0_ffn_W_down):
    import concourse.bacc as bacc
    import numpy as np
    from concourse.bass_utils import run_bass_kernel_spmd

    def c(a):
        return np.ascontiguousarray(a)

    def by_row(w):
        w = np.asarray(w)
        return w.reshape(-1, P, w.shape[-1]).transpose(1, 0, 2).reshape(P, -1)

    ctx_2048 = np.asarray(ctx_2048)
    wi, wu = (np.asarray(w).reshape(NCH, P, DT, P).transpose(3, 0, 2, 1).reshape(P, NCH, DT * P)
              for w in (L0_ffn_W_in_base, L0_ffn_W_up_base))
    wd = np.asarray(L0_ffn_W_down).T.reshape(NCH, P, D).transpose(1, 0, 2)
    arrays = {
        "x": c(np.asarray(x).reshape(T, D)),
        "ids": c(np.asarray(itok_BxS_13_99985).reshape(NT, P).T),
        "wexp": c(np.stack([by_row(ctx_2048[e].T) for e in range(E)], 1)),
        "wov": c(np.stack([by_row(L0_ffn_Wo), by_row(L0_ffn_Wv)], 1)),
        "amat": c(by_row(L0_ffn_A).reshape(P, DT, R)),
        "bmat": c(np.asarray(L0_ffn_B)),
        "ln": c(np.stack([np.asarray(w).reshape(DT, P).T for w in (L0_ffn_ln1_w, L0_ffn_ln2_w)], 1)),
        "gates": c(np.stack([np.asarray(g_xattn), np.asarray(g_ffn)], 1)),
        "wqk": c(np.stack([by_row(np.asarray(w).T) for w in (L0_ffn_Wq, L0_ffn_Wk)], 1)),
        "wmlp": c(np.concatenate([wi, wu, wd], 2)),
    }
    nc = bacc.Bacc("TRN2", target_bir_lowering=False, num_devices=1)
    args = {n: nc.dram_tensor(f"in_{n}", a.shape, mybir.dt.from_np(a.dtype), kind="ExternalInput").ap()
            for n, a in arrays.items()}
    out = nc.dram_tensor("out", [T, D], F32, kind="ExternalOutput").ap()
    build(nc, **args, out=out)
    got = run_bass_kernel_spmd(nc, [{f"in_{n}": a for n, a in arrays.items()}], core_ids=[0]).results[0]["out"]
    return got.reshape(NB, S, D)
```

```python
from contextlib import ExitStack

import concourse.bass as bass
from concourse import mybir

F32 = mybir.dt.float32
F32R = mybir.dt.float32r
I32 = mybir.dt.int32
ALU = mybir.AluOpType
ACT = mybir.ActivationFunctionType
AXX = mybir.AxisListType.X

P = 128
NB, S, D = 4, 512, 512
T = NB * S
DT = D // P
TT = S // P
NT = T // P
E = 4
PER_EXPERT = 25000 // E
ITEMS = T // P + E - 1
EW = DT * D
H, HD, R = 16, 32, 16
QH = P // HD
NQ = H // QH
F = 2048
NCH = F // P
CW = 2 * DT * P
LN_EPS, RMS_EPS = 1e-5, 1e-6
MASKED = -1e30
SCALE = float(HD) ** -0.5
MOD_SCALE = 0.1
HI, LO = 0, 1
Q_LO, Q_HI, K_HI, K_LO = range(4)
GATE, UP, Y0, QKB, ATT = 0, 1, 2, 3, 7
SCORE = {3: (0, 0, 0), 2: (1, 0, 512), 0: (1, 384, 896), 1: (2, 0, 1024)}
ROWS = (6, 7, 0, 1)
FIRST_QK = (6, 7)
VALUES, LOW_RANK = (4, 5), 0
TURNED = {0: (4, 0, 0), 1: (5, 0, 512), 3: (5, 384, 896), 2: (6, 0, 1024)}
PACKED = 1280
NORM_DVE, NORM_ACT = (3, 2, 1), (0,)
LOADS = 4
K_LN = 2 * TT + (13 + 12) + TT
NORM_AT = 4
PARTS = ((HI, HI), (LO, HI), (HI, LO))


def build(nc, x, ids, wexp, wov, amat, bmat, ln, gates, wqk, wmlp, out):
    ctx = ExitStack()
    with ctx:
        def sb(name, shape, dt=F32):
            return ctx.enter_context(nc.sbuf_tensor(name, shape, dt))

        def sem(name):
            return ctx.enter_context(nc.semaphore(name))

        xs = nc.dram_tensor("x_sorted", [T + P, D], F32).ap()
        res = nc.dram_tensor("residual", [T, D], F32).ap()
        ys = nc.dram_tensor("y_sorted", [T + P, D], F32).ap()

        big = sb("big", [P, NT, D])
        xt = big[:, 0:4, :]
        hb = big[:, 4:8, :]
        flat = big[:, :, :].rearrange("p a b -> p (a b)")
        x1 = big[:, 8:12, :]
        x1f = flat[:, 4096:4096 + TT * D]
        hbf = flat[:, 2048:2048 + TT * D]
        prob = [flat[:, 4096 + PACKED * k:4096 + PACKED * (k + 1)] for k in range(2)]
        vp = flat[:, 6656:6656 + TT * H * R].rearrange("p (t h r) -> p t h r", t=TT, h=H)
        stream = sb("stream", [P, 2, EW])
        wstage = sb("wstage", [P, 2, EW])
        wr = sb("wr", [P, 2, E * EW], F32R)
        wrf = wr[:, :, :].rearrange("p a b -> p (a b)")

        def carve(start, n):
            return wrf[:, start:start + n]

        hT = carve(0, 4096).rearrange("p (a d t) -> p a d t", a=2, d=DT)
        wqs = carve(4096, 2048).rearrange("p (a m d c) -> p a m d c", a=2, m=2, d=DT)
        qk = carve(6144, 2048).rearrange("p (m t) -> p m t", m=4)
        pts = carve(8192, 4 * PACKED).rearrange("p (h a c) -> p h a c", h=2, a=2)
        VS = QH * 64 + 64
        vst = carve(8192 + 4 * PACKED, TT * VS).rearrange("p (t c) -> p t c", t=TT)
        vst_v = vst[:, :, 0:QH * 64].rearrange("p t (h c) -> p t h c", h=QH)
        wqk_v = wstage[:, :, :].rearrange("p m (d c) -> p m d c", d=DT)
        braw = flat[0:96, 6144:6144 + F]
        stack = sb("stack", [3 * HD, 2, 2, S], F32R)
        vw = sb("vw", [P, 2, DT, H * R], F32R)
        apad = sb("apad", [P, DT, P], F32R)
        zst = sb("zst", [96, S], F32R)
        bst = sb("bst", [96, F], F32R)
        identr = sb("identr", [P, P], F32R)
        maskr = sb("maskr", [P, P], F32R)
        zeror = sb("zeror", [P, P], F32R)
        wch = sb("wch", [P, 2, 2, CW + D], F32R)
        actr = sb("actr", [P, 2, 2, S], F32R)
        xTs, aTs = actr[:, 0], actr[:, 1]
        ident = sb("ident", [P, P])
        tri = sb("tri", [P, P])
        ones = sb("ones", [P, P])
        xi = sb("xi", [P, D])
        sil = sb("sil", [P, S])
        act_sb = sb("act_sb", [P, S])
        ysb = sb("ysb", [P, D])
        araw = sb("araw", [P, DT, R])
        lns = sb("lns", [P, 2, DT])
        gt = sb("gt", [P, 2])
        tg = sb("tg", [P, 2])
        warm = sb("warm", [P, 1])
        bd = sb("bd", [P, DT, QH, R])
        idst = sb("idst", [P, NT], I32)
        idf = sb("idf", [P, NT])
        ge = sb("ge", [P, E + 1, NT])
        oh = sb("oh", [P, E, NT])
        cnt = sb("cnt", [P, 2, E * NT])
        cum = sb("cum", [P, E * NT])
        exc = sb("exc", [P, E * NT])
        pe_ = sb("pe_", [P, E, NT])
        posf = sb("posf", [P, NT])
        pos = sb("pos", [P, NT], I32)
        small = sb("small", [P, 16, E])
        lna = sb("lna", [P, NT])
        lnb = sb("lnb", [P, NT])
        bchunk = sb("bchunk", [96, 2, P], F32R)
        asc = sb("asc", [P, DT, R])
        nti = sb("nti", [P, E], I32)
        itf = sb("itf", [P, 20])
        its = sb("its", [P, 3, 20])
        itab = sb("itab", [P, 2, 20], I32)
        st = sb("st", [P, 8 * 6])
        mv = sb("mv", [P, 8, 2])
        nr = sb("nr", [P, 8 * 8])
        nri = sb("nri", [P, 8], I32)
        nb = sb("nb", [P, 4])
        rs = sb("rs", [P, 2, 4])
        rr = sb("rr", [P, 2, 4])
        haT, att_low, att_sum, zrow = xi[0:R, :], ysb[0:R, :], act_sb[0:R, :], sil[0:R, :]

        bank = [ctx.enter_context(nc.psum_tensor(f"bank{k}", [P, 512], F32)) for k in range(8)]

        ids_in, small_in, wov_in, wqk_in = sem("ids_in"), sem("small_in"), sem("wov_in"), sem("wqk_in")
        b_in = sem("b_in")
        x_in = [sem(f"x_in{g}") for g in range(4)]
        exp_in = [sem(f"exp_in{k}") for k in range(2)]
        exp_hi, exp_lo = sem("exp_hi"), sem("exp_lo")
        const_ok, zero_ok, tail_ok = sem("const_ok"), sem("zero_ok"), sem("tail_ok")
        pool_own, dve_own, act_own = sem("pool_own"), sem("dve_own"), sem("act_own")
        onehot_ok, ranks_ok, pos_ok, items_ok = sem("onehot_ok"), sem("ranks_ok"), sem("pos_ok"), sem("items_ok")
        norm_ok, xn_ok, scattered = sem("norm_ok"), sem("xn_ok"), sem("scattered")
        woa_ok, bd_ok, vw_mm, vw_hi, prep_ok = sem("woa_ok"), sem("bd_ok"), sem("vw_mm"), sem("vw_hi"), sem("prep_ok")
        tanh_ok, wqk_ok = sem("tanh_ok"), sem("wqk_ok")
        xi_in, x_turned, xt_hi, xt_lo = sem("xi_in"), sem("x_turned"), sem("xt_hi"), sem("xt_lo")
        h_done, h_silu, h_gated = sem("h_done"), sem("h_silu"), sem("h_gated")
        a_turned, at_hi, at_lo = sem("a_turned"), sem("at_hi"), sem("at_lo")
        y_done, y_copied, y_stored = sem("y_done"), sem("y_copied"), sem("y_stored")
        y_first = [sem(f"y_first{k}") for k in range(TT)]
        x1_in, y_in, res_out, res_in = sem("x1_in"), sem("y_in"), sem("res_out"), sem("res_in")
        ln_ok, hb_ok = sem("ln_ok"), sem("hb_ok")
        hb_turned, ht_hi, ht_lo = sem("hb_turned"), sem("ht_hi"), sem("ht_lo")
        vp_done, vp_copied = sem("vp_done"), sem("vp_copied")
        ha_done, ha_low, ha_ok = sem("ha_done"), sem("ha_low"), sem("ha_ok")
        wq_hi, wq_lo = sem("wq_hi"), sem("wq_lo")
        qk_done, qk_hi, qk_lo = sem("qk_done"), sem("qk_hi"), sem("qk_lo")
        stk = [sem(f"stk{k}") for k in range(2)]
        vst_hi, vst_lo = sem("vst_hi"), sem("vst_lo")
        s_done, nb_ok, exp_ok = sem("s_done"), sem("nb_ok"), sem("exp_ok")
        pn_ok, pn_act = sem("pn_ok"), sem("pn_act")
        p_turned, pt_hi, pt_lo, pv_done = sem("p_turned"), sem("pt_hi"), sem("pt_lo"), sem("pv_done")
        at_low, at_sum, mod_ok, z_ok, zs_hi, zs_ok = (sem(n) for n in ("at_low", "at_sum", "mod_ok", "z_ok", "zs_hi", "zs_ok"))
        cg_in = [sem(f"cg_in{k}") for k in range(2)]
        cd_in = [sem(f"cd_in{k}") for k in range(2)]
        cg_hi, cg_lo, cd_hi, cd_lo = (sem(n) for n in ("cg_hi", "cg_lo", "cd_hi", "cd_lo"))
        apad_ok, bst_ok, vst_zero, rr_ok, ln_own = (sem(n) for n in ("apad_ok", "bst_ok", "vst_zero", "rr_ok", "ln_own"))
        g_done, u_done, g_silu, gu_ok, gu_hi, gu_lo = (sem(n) for n in ("g_done", "u_done", "g_silu", "gu_ok", "gu_hi", "gu_lo"))
        d_done, fin_out, out_in = sem("d_done"), sem("fin_out"), sem("out_in")

        def prob_rows(par, qt):
            at = SCORE[qt][2]
            return prob[par][:, at:at + P * (qt + 1)]

        def gu_view(cols):
            return cols.rearrange("p (m d f) -> p m d f", m=2, d=DT)

        def loads_of(b, c):
            half = c // 2
            return b * (16 * NCH // 2) + half * 16 + 16

        x_tiles = x.rearrange("(g j p) d -> g p j d", p=P, j=4)
        out_tiles = out.rearrange("(g j p) d -> g p j d", p=P, j=4)
        res_tiles = res.rearrange("(g j p) d -> g p j d", p=P, j=4)

        block = ctx.enter_context(nc.Block())

        @block.sync
        def _(sp):
            sp.dma_start(idst[:, :], ids).then_inc(ids_in, 16)
            for g in range(4):
                sp.dma_start(big[:, 4 * g:4 * g + 4, :], x_tiles[g]).then_inc(x_in[g], 16)
                if g == 1:
                    sp.dma_start(lns[:, :, :], ln).then_inc(small_in, 16)
                    sp.dma_start(gt[:, :], gates.broadcast_to([P, 2])).then_inc(small_in, 16)
                    sp.dma_start(araw[:, :, :], amat).then_inc(small_in, 16)
            for e in range(2):
                sp.dma_start(stream[:, e, :], wexp[:, e, :]).then_inc(exp_in[e], 16)
            for e in range(2, E):
                sp.wait_ge(exp_hi, e - 1)
                sp.wait_ge(exp_lo, e - 1)
                sp.dma_start(stream[:, e % 2, :], wexp[:, e, :]).then_inc(exp_in[e % 2], 16)
            sp.wait_ge(zero_ok, 1)
            sp.dma_start(xs[T:T + P, :], ysb[:, :]).then_inc(tail_ok, 16)
            sp.wait_ge(tail_ok, 16)
            def item_rows(i):
                sp.wait_ge(items_ok, 1)
                return sp.value_load(itab[0:1, 0, bass.ds(i, 1)], min_val=0, max_val=T)

            def load_item(i):
                sp.dma_start(xi[:, :], xs[bass.ds(item_rows(i), P), :]).then_inc(xi_in, 16)

            def store_item(i):
                rows = item_rows(i)
                sp.wait_ge(y_copied, i + 1)
                sp.dma_start(ys[bass.ds(rows, P), :], ysb[:, :]).then_inc(y_stored, 16)

            sp.wait_ge(items_ok, 1)
            sp.wait_ge(scattered, 16 * NT)
            load_item(0)
            for i in range(1, 3):
                sp.wait_ge(x_turned, i)
                load_item(i)
            sp.wait_ge(bst_ok, 1)
            for k in range(3):
                sp.dma_start(braw[32 * k:32 * k + R, :], bmat).then_inc(b_in, 16)

            def next_item(i):
                sp.wait_ge(x_turned, i)
                load_item(i)
                store_item(i - 3)

            sp.wait_ge(exp_hi, E)
            sp.wait_ge(exp_lo, E)
            for first, dst, src, landed in ((3, stream, wov, wov_in), (3 + LOADS, wstage, wqk, wqk_in)):
                to = dst[:, :, :].rearrange("p a b -> p (a b)")
                cols = src.rearrange("p a b -> p (a b)")
                with sp.Fori(first, first + LOADS) as i:
                    next_item(i)
                    at = (i - first) * (2 * EW // LOADS)
                    sp.dma_start(to[:, bass.ds(at, 2 * EW // LOADS)],
                                 cols[:, bass.ds(at, 2 * EW // LOADS)]).then_inc(landed, 16)
            with sp.Fori(3 + 2 * LOADS, ITEMS) as i:
                next_item(i)
            sp.dma_start(x1, x_tiles[0]).then_inc(x1_in, 16)
            for i in range(ITEMS - 3, ITEMS):
                store_item(i)

            def load_chunk(b, c, par, first=False):
                if not first:
                    sp.wait_ge(cg_lo, b * NCH + c - 1)
                sp.dma_start(stream[:, par, 0:CW], wmlp[:, bass.ds(c, 1), 0:CW]).then_inc(cg_in[par], 16)
                if not first:
                    sp.wait_ge(cd_lo, b * NCH + c - 1)
                sp.dma_start(stream[:, par, CW:CW + D], wmlp[:, bass.ds(c, 1), CW:CW + D]).then_inc(cd_in[par], 16)

            def load_stack(b, q, j):
                g = b * NQ + q
                if j == 0:
                    sp.wait_ge(qk_lo, g * 2 + 2)
                elif type(q) is int and j == 1:
                    pass
                else:
                    sp.wait_ge(s_done, g * (3 * QH) + (j - 1) * 3)
                rows = slice(HD * j, HD * j + HD)
                for k, (a, c) in enumerate(((Q_HI, K_HI), (Q_LO, K_HI), (Q_HI, K_LO))):
                    sp.dma_start(stack[HD * k:HD * k + HD, j % 2, :, :].bitcast(F32),
                                 qk[rows, a:c + 1:c - a, :].bitcast(F32)).then_inc(stk[j % 2], 16)

            def load_x(b):
                rows = x_tiles[bass.ds(b, 1)]
                sp.wait_ge(p_turned, b * (H * 3))
                sp.dma_start(x1, rows).then_inc(x1_in, 16)

            def store_residual(b):
                rows = res_tiles[bass.ds(b, 1)]
                sp.wait_ge(ln_own, (b + 1) * K_LN)
                sp.dma_start(rows, x1).then_inc(res_out, 16)
                sp.wait_ge(res_out, (b + 1) * 16)

            def load_residual(b, first=False):
                rows = res_tiles[bass.ds(b, 1)]
                if not first:
                    sp.wait_ge(out_in, b * 16)
                sp.dma_start(xt, rows).then_inc(res_in, 16)

            def batch(b, more, first=False):
                for j in range(2):
                    load_stack(b, 0, j)
                if not first:
                    load_residual(b)
                for c in range(2):
                    load_chunk(b, c, c, first=True)
                for j in range(2, QH):
                    load_stack(b, 0, j)
                with sp.Fori(1, NQ) as q:
                    for j in range(QH):
                        load_stack(b, q, j)
                if more:
                    load_x(b + 1)
                with sp.Fori(1, NCH // 2) as c2:
                    for par in range(2):
                        load_chunk(b, c2 * 2 + par, par)
                if more:
                    store_residual(b + 1)
                if more:
                    rows = out_tiles[bass.ds(b, 1)]
                    sp.wait_ge(fin_out, b + 2)
                    sp.dma_start(rows, xt).then_inc(out_in, 16)
                else:
                    for tt in range(TT):
                        sp.wait_ge(fin_out, b + 2 + tt)
                        sp.dma_start(out_tiles[b, :, tt, :], xt[:, tt, :]).then_inc(out_in, 16)

            sp.wait_ge(vw_mm, 2)
            store_residual(0)
            load_residual(0, first=True)
            batch(0, True, first=True)
            with sp.Fori(1, NB - 1) as b:
                batch(b, True)
            batch(NB - 1, False)
            sp.wait_ge(out_in, (NB - 1 + TT) * 16)
            sp.wait_ge(y_stored, ITEMS * 16)

        @block.gpsimd
        def _(pool):
            g = nc.gpsimd
            g.memset(ysb[:, :], 0.0).then_inc(zero_ok, 1)
            g.memset(ident[:, :], 0.0).then_inc(pool_own, 1)
            g.memset(ones[:, :], 1.0).then_inc(pool_own, 1)
            g.memset(act_sb[:, :], 0.0).then_inc(pool_own, 1)
            g.memset(zeror[:, :].bitcast(F32), 0.0).then_inc(pool_own, 1)
            g.memset(apad[:, :, :].bitcast(F32), 0.0).then_inc(pool_own, 1)
            g.iota(itab[:, 0, :], [[1, 20]], base=0, channel_multiplier=0).then_inc(pool_own, 1)
            pool.wait_ge(pool_own, 6)
            g.affine_select(out=ident[:, :], in_=ident[:, :], compare_op=ALU.not_equal, fill=1.0,
                            base=0, pattern=[[-1, P]], channel_multiplier=1).then_inc(const_ok, 1)
            g.affine_select(out=tri[:, :], in_=ones[:, :], compare_op=ALU.is_gt, fill=0.0,
                            base=0, pattern=[[1, P]], channel_multiplier=-1).then_inc(const_ok, 1)
            g.affine_select(out=act_sb[:, 0:P], in_=act_sb[:, 0:P], compare_op=ALU.is_ge, fill=MASKED,
                            base=0, pattern=[[-1, P]], channel_multiplier=1).then_inc(const_ok, 1)
            g.tensor_copy(itf[:, :], itab[:, 0, :]).then_inc(const_ok, 1)
            pool.wait_ge(const_ok, 4)
            g.tensor_copy(identr[:, :], ident[:, :]).then_inc(const_ok, 1)
            g.tensor_copy(maskr[:, :], act_sb[:, 0:P]).then_inc(const_ok, 1)
            pool.wait_ge(pos_ok, 1)
            for t in range(NT):
                pool.wait_ge(xn_ok, t + 1)
                g.indirect_dma_start(xs[0:T, :], bass.IndirectOffsetOnAxis(ap=pos[:, t:t + 1], axis=0),
                                     big[:, t, :], None).then_inc(scattered, 16)
            pool.wait_ge(scattered, 16 * NT)
            g.memset(braw, 0.0).then_inc(bst_ok, 1)
            pool.wait_ge(small_in, 48)
            for dt in range(DT):
                ins = g.tensor_scalar(asc[:, dt, :], araw[:, dt, :], lns[:, 1, dt:dt + 1], None, ALU.mult)
            ins.then_inc(pool_own, 1)
            pool.wait_ge(pool_own, 7)
            g.tensor_copy(apad[:, :, 0:R], asc[:, :, :]).then_inc(pool_own, 1)
            pool.wait_ge(pool_own, 8)
            g.tensor_tensor(apad[:, :, 32:32 + R], asc[:, :, :], apad[:, :, 0:R].bitcast(F32),
                            ALU.subtract).then_inc(apad_ok, 1)
            pool.wait_ge(b_in, 48)
            g.tensor_copy(bst[:, :], braw).then_inc(pool_own, 1)
            pool.wait_ge(pool_own, 9)
            g.tensor_tensor(bst[64:96, :], braw[64:96, :], bst[64:96, :].bitcast(F32),
                            ALU.subtract).then_inc(bst_ok, 1)

            pool.wait_ge(bst_ok, 2)
            pool.wait_ge(y_stored, 16 * ITEMS)

            def gather(b):
                for t in range(b * TT, (b + 1) * TT):
                    landed = y_in if b else y_first[t]
                    g.indirect_dma_start(hb[:, t % TT, :], None, ys[0:T, :],
                                         bass.IndirectOffsetOnAxis(ap=pos[:, t:t + 1], axis=0)).then_inc(landed, 16)

            def low(dst, src, high, done):
                g.tensor_tensor(dst, src, high.bitcast(F32), ALU.subtract).then_inc(done, 1)

            def weights_low(b, q):
                src = wqk_v[:, :, :, bass.ds(q * P, P)]
                pool.wait_ge(wq_hi, b * NQ + q + 1)
                low(wqs[:, LO, :, :, :], src, wqs[:, HI, :, :, :], wq_lo)

            gather(0)
            for b in range(NB):
                for q in range(0 if b == 0 else 1, NQ):
                    weights_low(b, q)
                if b < NB - 1:
                    pool.wait_ge(hb_turned, (b + 1) * TT)
                    gather(b + 1)
                    weights_low(b + 1, 0)

        @block.tensor
        def _(pe):
            def split_product(dst, lhs, rhs, tiles, start=True, stop=True, skip=False):
                n = len(PARTS) * tiles
                i = 0
                for k in range(tiles):
                    for pl, pr in PARTS:
                        mm = pe.matmul(dst, lhs(pl, k), rhs(pr, k), start=start and i == 0,
                                       stop=stop and i == n - 1, skip_group_check=skip)
                        i += 1
                return mm

            pe.wait_ge(const_ok, 6)
            pe.wait_ge(onehot_ok, 1)
            ohf = oh[:, :, :].rearrange("p e t -> p (e t)")
            pe.matmul(bank[0][:, 0:64], tri[:, :], ohf, start=True, stop=True)
            pe.matmul(bank[0][:, 64:128], ones[:, :], ohf, start=True, stop=True).then_inc(ranks_ok, 1)

            XB, HB, AB, YB = 4, 5, 6, 7

            def turn_x(i, first=False):
                pe.wait_ge(xi_in, i * 16 + 16)
                if not first:
                    pe.wait_ge(xt_lo, i)
                for k in range(DT):
                    mm = pe.transpose(bank[XB][:, k * P:k * P + P], xi[:, k * P:k * P + P], ident[:, :])
                mm.then_inc(x_turned, 1)

            def first_product(w, i, first=False):
                pe.wait_ge(xt_lo, i + 1)
                if not first:
                    pe.wait_ge(h_gated, i)
                split_product(bank[HB][:, :], lambda p, k: xTs[:, p, k * P:k * P + P],
                              lambda p, k: wr[:, p, bass.ds(w + k * D, D)], DT).then_inc(h_done, 1)

            def turn_act(i, first=False):
                pe.wait_ge(h_gated, i + 1)
                if not first:
                    pe.wait_ge(at_lo, i)
                for k in range(DT):
                    mm = pe.transpose(bank[AB][:, k * P:k * P + P], act_sb[:, k * P:k * P + P], ident[:, :])
                mm.then_inc(a_turned, 1)

            def second_product(w, i, first=False):
                pe.wait_ge(at_lo, i + 1)
                if not first:
                    pe.wait_ge(y_copied, i)
                split_product(bank[YB][:, :], lambda p, k: aTs[:, p, k * P:k * P + P],
                              lambda p, k: wr[:, p, bass.ds(w + k * D, D)], DT).then_inc(y_done, 1)

            def weight_of(i):
                return pe.value_load(itab[0:1, 1, bass.ds(i, 1)], min_val=0, max_val=(E - 1) * EW)

            pe.wait_ge(items_ok, 1)
            pe.wait_ge(exp_hi, E)
            pe.wait_ge(exp_lo, E)
            turn_x(0, first=True)
            first_product(weight_of(0), 0, first=True)
            turn_x(1)
            turn_act(0, first=True)
            first_product(weight_of(1), 1)
            turn_x(2)
            second_product(weight_of(0), 0, first=True)
            turn_act(1)
            with pe.Fori(2, ITEMS - 1) as i:
                first_product(weight_of(i), i)
                turn_x(i + 1)
                second_product(weight_of(i - 1), i - 1)
                turn_act(i)
            last = ITEMS - 1
            first_product(weight_of(last), last)
            second_product(weight_of(last - 1), last - 1)
            turn_act(last)
            second_product(weight_of(last), last)

            pe.wait_ge(wov_in, 16 * LOADS)
            pe.wait_ge(small_in, 48)
            for ct in range(DT):
                for dt in range(DT):
                    mm = pe.matmul(bank[1][:, ct * R:ct * R + R],
                                   stream[:, 0, dt * D + ct * P:dt * D + ct * P + P], araw[:, dt, :],
                                   start=dt == 0, stop=dt == DT - 1)
            mm.then_inc(woa_ok, 1)
            pe.wait_ge(bd_ok, 1)
            for dt in range(DT):
                for ct in range(DT):
                    mm = pe.matmul(bank[2 + dt // 2][:, 256 * (dt % 2) + 64 * ct:256 * (dt % 2) + 64 * ct + 64],
                                   stream[:, 1, ct * D + dt * P:ct * D + dt * P + P],
                                   bd[:, ct, :, :].rearrange("p h r -> p (h r)"), start=True, stop=True)
                if dt % 2:
                    mm.then_inc(vw_mm, 1)

            pe.wait_ge(prep_ok, 1)
            pe.wait_ge(apad_ok, 1)

            def turn_rows(b, tiles):
                pe.wait_ge(hb_ok, b * TT + TT)
                for dt in tiles:
                    for tt in range(TT):
                        mm = pe.transpose(bank[ROWS[dt]][:, tt * P:tt * P + P], hb[:, tt, dt * P:dt * P + P],
                                          ident[:, :])
                    mm.then_inc(hb_turned, 1)

            def project(b, q, which, to=QKB, half=None):
                n = b * NQ + q
                if half != 1:
                    pe.wait_ge(wq_hi, n + 1)
                    pe.wait_ge(wq_lo, n + 1)
                    if which and to == QKB:
                        pe.wait_ge(qk_lo, n * 2 + 1)
                tiles = DT if half is None else DT // 2
                at = tiles if half == 1 else 0
                mm = split_product(bank[to][:, :], lambda p, k: wqs[:, p, which, at + k, :],
                                   lambda p, k: hT[:, p, at + k, :], tiles,
                                   start=half != 1, stop=half != 0, skip=half is not None)
                if half != 0:
                    mm.then_inc(qk_done, 1)

            def scores(n, par, loads, first=False):
                pe.wait_ge(stk[par], loads)
                if not first:
                    pe.wait_ge(exp_ok, n * 4)
                for i, qt in enumerate((3, 2, 0, 1)):
                    bk, col, _ = SCORE[qt]
                    w = P * (qt + 1)
                    pe.matmul(bank[bk][:, col:col + w], stack[:, par, 0, qt * P:qt * P + P],
                              stack[:, par, 1, 0:w], start=True, stop=False, skip_group_check=True)
                    mm = pe.matmul(bank[bk][:, col + w - P:col + w], identr[:, :], maskr[:, :],
                                   start=False, stop=True, skip_group_check=True)
                    if qt != 2:
                        mm.then_inc(s_done, 1)

            def turn_probs(n, par, first=False):
                pe.wait_ge(pn_ok, (n + 1) * len(NORM_DVE))
                pe.wait_ge(pn_act, (n + 1) * len(NORM_ACT))
                for kt in (0, 1, 3, 2):
                    bk, col, _ = TURNED[kt]
                    if not first and kt != 3:
                        pe.wait_ge(pt_lo, (n - 1) * 3 + (1, 2, 3)[kt])
                    for qt in range(kt, TT):
                        src = SCORE[qt][2] + kt * P
                        mm = pe.transpose(bank[bk][:, col + (qt - kt) * P:col + (qt - kt) * P + P],
                                          prob[par][:, src:src + P], ident[:, :])
                    if kt != 1:
                        mm.then_inc(p_turned, 1)

            def attend(b, q, n, j):
                pe.wait_ge(pt_lo, n * 3 + 3)
                pe.wait_ge(vst_lo, b * NQ + q + 1)
                for kt in range(TT):
                    _, _, at = TURNED[kt]
                    w = S - kt * P
                    for part in (HI, LO):
                        mm = pe.matmul(bank[ATT][:, kt * P:S], vst[:, kt, 64 * j:64 * j + P],
                                       pts[:, j % 2, part, at:at + w], start=False, stop=False, skip_group_check=True)
                mm.then_inc(pv_done, 1)

            def head_step(b, q, j, ahead):
                n = (b * NQ + q) * QH + j
                if j == 2 and ahead == 2:
                    project(b, q + 2, 0, half=0)
                if j == 0 and ahead:
                    project(b, q + 1, 1)
                if j == 3 and ahead == 2:
                    project(b, q + 2, 0, half=1)
                if ahead or j < QH - 1:
                    turn_probs(n + 1, (j + 1) % 2)
                if ahead or j < QH - 3:
                    m = b * (H // 2) + q * 2 + (j + 3) // 2
                    scores(n + 3, (j + 1) % 2, m * 48 + 48)
                attend(b, q, n, j)

            def gate_product(par):
                split_product(bank[GATE][:, :], lambda p, k: wch[:, par, p, k * P:k * P + P],
                              lambda p, k: hT[:, p, k, :], DT, stop=False)

            def modulate(par):
                pe.matmul(bank[GATE][:, :], bchunk[:, par, :], zst[:, :], start=False,
                          stop=True).then_inc(g_done, 1)

            def up_product(par):
                split_product(bank[UP][:, :], lambda p, k: wch[:, par, p, (DT + k) * P:(DT + k) * P + P],
                              lambda p, k: hT[:, p, k, :], DT).then_inc(u_done, 1)

            def gate_up(b, c, par):
                n = b * NCH + c
                pe.wait_ge(cg_hi, n + 1)
                pe.wait_ge(cg_lo, n + 1)
                pe.wait_ge(gu_ok, n)
                gate_product(par)
                modulate(par)
                up_product(par)

            def down(b, c, par, by_tile=False):
                n = b * NCH + c
                pe.wait_ge(gu_lo, n + 1)
                pe.wait_ge(cd_lo, n + 1)
                for tt in range(TT):
                    mm = split_product(bank[Y0 + tt][:, :], lambda p, k: actr[:, par, p, tt * P:tt * P + P],
                                       lambda p, k: wch[:, par, p, CW:CW + D], 1, start=False, stop=False, skip=True)
                    if by_tile or tt == TT - 1:
                        mm.then_inc(d_done, 1)

            def batch(b, more):
                pe.wait_ge(ht_lo, b * 4 + 4)
                for which in range(2):
                    project(b, 0, which, FIRST_QK[which])
                for k in range(DT):
                    for part in (HI, LO):
                        mm = pe.matmul(bank[LOW_RANK][:, :], apad[:, k, :], hT[:, part, k, :],
                                       start=k == 0 and part == HI, stop=k == DT - 1 and part == LO)
                mm.then_inc(ha_done, 1)
                pe.wait_ge(fin_out, b + 1)
                for tt in range(TT):
                    mm = split_product(bank[VALUES[tt // 2]][:, 256 * (tt % 2):256 * (tt % 2) + 256],
                                       lambda p, k: hT[:, p, k, tt * P:tt * P + P],
                                       lambda p, k: vw[:, p, k, :], DT)
                    if tt % 2:
                        mm.then_inc(vp_done, 1)
                pe.wait_ge(ha_ok, b + 1)
                pe.wait_ge(qk_lo, b * (NQ * 2) + 2)
                pe.matmul(bank[ATT][:, :], zeror[:, :], hT[:, HI, 0, :], start=True, stop=False,
                          skip_group_check=True).then_inc(pv_done, 1)
                scores(b * H, 0, b * (H // 2) * 48 + 48, first=True)
                project(b, 1, 0)
                scores(b * H + 1, 1, b * (H // 2) * 48 + 48)
                pe.wait_ge(vp_copied, b * 2 + 2)
                turn_probs(b * H, 0, first=True)
                scores(b * H + 2, 0, b * (H // 2) * 48 + 96)
                with pe.Fori(0, NQ - 2) as q:
                    for j in range(QH):
                        head_step(b, q, j, 2)
                for q, ahead in ((NQ - 2, 1), (NQ - 1, 0)):
                    for j in range(QH):
                        head_step(b, q, j, ahead)
                pe.wait_ge(exp_ok, (b + 1) * H * 4)
                pe.wait_ge(cg_hi, b * NCH + 1)
                pe.wait_ge(cg_lo, b * NCH + 1)
                up_product(0)
                for tt in range(TT):
                    pe.matmul(bank[Y0 + tt][:, :], zeror[:, :], hT[:, HI, 0, :], start=True, stop=False,
                              skip_group_check=True)
                gate_product(0)
                pe.wait_ge(zs_ok, b + 1)
                modulate(0)
                with pe.Fori(0, NCH // 2 - 1) as c2:
                    gate_up(b, c2 * 2 + 1, 1)
                    down(b, c2 * 2, 0)
                    gate_up(b, c2 * 2 + 2, 0)
                    down(b, c2 * 2 + 1, 1)
                gate_up(b, NCH - 1, 1)
                if more:
                    turn_rows(b + 1, (0, 1))
                down(b, NCH - 2, 0)
                if more:
                    pe.wait_ge(gu_ok, (b + 1) * NCH)
                    turn_rows(b + 1, (2, 3))
                down(b, NCH - 1, 1, by_tile=not more)

            for tt in range(TT):
                pe.wait_ge(hb_ok, tt + 1)
                for dt in range(DT):
                    mm = pe.transpose(bank[ROWS[dt]][:, tt * P:tt * P + P], hb[:, tt, dt * P:dt * P + P], ident[:, :])
                    if tt == TT - 1:
                        mm.then_inc(hb_turned, 1)
            with pe.Fori(0, NB - 1) as b:
                batch(b, True)
            batch(NB - 1, False)

        @block.scalar
        def _(act):
            a = nc.scalar

            def copy(dst, src):
                return a.activation(dst, src, ACT.Copy)

            act.wait_ge(small_in, 48)
            a.activation(tg[:, :], gt[:, :], ACT.Tanh).then_inc(tanh_ok, 1)
            def expert_high(e):
                act.wait_ge(exp_in[e % 2], 16 * (e // 2 + 1))
                copy(wr[:, HI, e * EW:(e + 1) * EW], stream[:, e % 2, :]).then_inc(exp_hi, 1)

            for half in range(2):
                for t in range(NT // 2 * half, NT // 2 * (half + 1)):
                    act.wait_ge(norm_ok, half + 1)
                    a.activation(big[:, t, :], big[:, t, :], ACT.Identity, bias=lnb[:, t:t + 1],
                                 scale=lna[:, t:t + 1]).then_inc(xn_ok, 1)
                if half == 0:
                    expert_high(0)
                    expert_high(1)
            expert_high(2)
            expert_high(3)

            def x_high(i, first=False):
                act.wait_ge(x_turned, i + 1)
                if not first:
                    act.wait_ge(h_done, i)
                copy(xTs[:, HI, :], bank[4][:, :]).then_inc(xt_hi, 1)

            def silu(i, first=False):
                act.wait_ge(h_done, i + 1)
                if not first:
                    act.wait_ge(h_gated, i)
                a.activation(sil[:, :], bank[5][:, :], ACT.Silu).then_inc(h_silu, 1)

            def act_high(i, first=False):
                act.wait_ge(a_turned, i + 1)
                if not first:
                    act.wait_ge(y_done, i)
                copy(aTs[:, HI, :], bank[6][:, :]).then_inc(at_hi, 1)

            def copy_y(i, first=False):
                act.wait_ge(y_done, i + 1)
                if first:
                    act.wait_ge(tail_ok, 16)
                else:
                    act.wait_ge(y_stored, i * 16)
                copy(ysb[:, :], bank[7][:, :]).then_inc(y_copied, 1)

            x_high(0, first=True)
            silu(0, first=True)
            x_high(1)
            act_high(0, first=True)
            silu(1)
            x_high(2)
            copy_y(0, first=True)
            act_high(1)
            with act.Fori(2, ITEMS - 1) as i:
                silu(i)
                x_high(i + 1)
                copy_y(i - 1)
                act_high(i)
            last = ITEMS - 1
            silu(last)
            copy_y(last - 1)
            act_high(last)
            copy_y(last)
            act.wait_ge(vw_mm, 2)
            for dt in range(DT):
                a.activation(vw[:, HI, dt, :], bank[2 + dt // 2][:, 256 * (dt % 2):256 * (dt % 2) + 256],
                             ACT.Copy, scale=lns[:, 0, dt:dt + 1]).then_inc(vw_hi, 1)

            def split_wqk(b, q):
                copy(wqs[:, HI, :, :, :], wqk_v[:, :, :, bass.ds(q * P, P)]).then_inc(wq_hi, 1)

            def split_qk(b, q, which, first=False, at=QKB):
                n = b * NQ + q
                act.wait_ge(qk_done, n * 2 + which + 1)
                if which == 0 and not first:
                    for k in range(2):
                        act.wait_ge(stk[k], n * 96)
                copy(qk[:, (Q_HI, K_HI)[which], :], bank[at][:, :]).then_inc(qk_hi, 1)

            def exponentials(n, par):
                for qt, maxima in ((3, 1), (2, 3), (0, 3), (1, 4)):
                    act.wait_ge(nb_ok, n * 4 + maxima)
                    bk, col, at = SCORE[qt]
                    w = P * (qt + 1)
                    a.activation(prob[par][:, at:at + w], bank[bk][:, col:col + w], ACT.Exp,
                                 bias=nb[:, qt:qt + 1], accum_out=rs[:, par, qt:qt + 1]).then_inc(exp_ok, 1)

            def normalise(n, par):
                act.wait_ge(rr_ok, n + 1)
                for qt in NORM_ACT:
                    rows = prob_rows(par, qt)
                    a.activation(rows, rows, ACT.Copy, scale=rr[:, par, qt:qt + 1]).then_inc(pn_act, 1)

            def head_step(b, q, j, ahead):
                n = (b * NQ + q) * QH + j
                if ahead or j < QH - 1:
                    exponentials(n + 1, (j + 1) % 2)
                    normalise(n + 1, (j + 1) % 2)
                if j < 2 and ahead:
                    split_qk(b, q + 1, j)
                for i, (bk, w, at) in enumerate(((4, 512, 0), (5, 512, 512), (6, 256, 1024))):
                    act.wait_ge(p_turned, n * 3 + i + 1)
                    copy(pts[:, j % 2, HI, at:at + w], bank[bk][:, 0:w]).then_inc(pt_hi, 1)
                if j == 0:
                    act.wait_ge(pv_done, b + 1 + n)
                    act.wait_ge(vp_copied, b * 2 + 2)
                    act.wait_ge(vst_zero, 1)
                    copy(vst_v[:, :, :, 0:R], vp[:, :, bass.ds(q * QH, QH), :]).then_inc(vst_hi, 1)

            def quad(b, q, ahead):
                for j in range(QH):
                    head_step(b, q, j, ahead)
                    if j == 1 and ahead == 2:
                        split_wqk(b, q + 2)

            def split_gate_up(b, c, par):
                act.wait_ge(cg_in[par], loads_of(b, c))
                raw, dst = gu_view(stream[:, par, 0:CW]), gu_view(wch[:, par, HI, 0:CW])
                for dt in range(DT):
                    ins = a.activation(dst[:, :, dt, :], raw[:, :, dt, :], ACT.Copy, scale=lns[:, 1, dt:dt + 1])
                ins.then_inc(cg_hi, 1)

            def chunk_step(b, c, par, more=True):
                n = b * NCH + c
                act.wait_ge(g_done, n + 1)
                a.activation(sil[:, :], bank[GATE][:, :], ACT.Silu).then_inc(g_silu, 1)
                act.wait_ge(cd_in[par], loads_of(b, c))
                copy(wch[:, par, HI, CW:CW + D], stream[:, par, CW:CW + D]).then_inc(cd_hi, 1)
                act.wait_ge(gu_ok, n + 1)
                copy(actr[:, par, HI, :], act_sb[:, :]).then_inc(gu_hi, 1)
                if more:
                    split_gate_up(b, c + 2, par)

            def norm_rows(b, j):
                act.wait_ge(ln_ok, b + 1)
                a.activation(hbf[:, bass.ds(j * D, D)], x1f[:, bass.ds(j * D, D)], ACT.Identity,
                             bias=lnb[:, bass.ds(j, 1)], scale=lna[:, bass.ds(j, 1)]).then_inc(hb_ok, 1)

            def rows_high(b):
                for dt in range(DT):
                    act.wait_ge(hb_turned, b * 4 + dt + 1)
                    copy(hT[:, HI, dt, :], bank[ROWS[dt]][:, :]).then_inc(ht_hi, 1)

            def batch(b, more):
                for which in range(2):
                    split_qk(b, 0, which, True, FIRST_QK[which])
                act.wait_ge(ha_done, b + 1)
                copy(att_low, bank[LOW_RANK][32:32 + R, :]).then_inc(ha_low, 1)
                split_wqk(b, 1)
                act.wait_ge(const_ok, 6)
                a.activation(warm[:, :], ones[:, 0:1], ACT.Exp).then_inc(act_own, 1)
                for k in range(2):
                    act.wait_ge(vp_done, b * 2 + k + 1)
                    copy(vp[:, 2 * k:2 * k + 2, :, :].rearrange("p t h r -> p (t h r)"),
                         bank[VALUES[k]][:, :]).then_inc(vp_copied, 1)
                act.wait_ge(res_out, (b + 1) * 16)
                exponentials(b * H, 0)
                normalise(b * H, 0)
                with act.Fori(0, NQ - 2) as q:
                    quad(b, q, 2)
                quad(b, NQ - 2, 1)
                for j in range(QH):
                    head_step(b, NQ - 1, j, 0)
                    if j == 1:
                        split_gate_up(b, 0, 0)
                split_gate_up(b, 1, 1)
                act.wait_ge(pv_done, (b + 1) * (H + 1))
                copy(att_low, bank[ATT][32:32 + R, :]).then_inc(at_low, 1)
                act.wait_ge(at_sum, b + 1)
                a.activation(att_low, att_sum, ACT.Tanh).then_inc(mod_ok, 1)
                act.wait_ge(z_ok, b + 1)
                copy(zst[0:R, :], zrow)
                copy(zst[64:64 + R, :], zrow).then_inc(zs_hi, 1)
                if more:
                    with act.Fori(0, NORM_AT) as c2:
                        for par in range(2):
                            chunk_step(b, c2 * 2 + par, par)
                    with act.Fori(NORM_AT, NORM_AT + 2) as c2:
                        for par in range(2):
                            chunk_step(b, c2 * 2 + par, par)
                            norm_rows(b + 1, c2 * 2 + par - 2 * NORM_AT)
                    with act.Fori(NORM_AT + 2, NCH // 2 - 1) as c2:
                        for par in range(2):
                            chunk_step(b, c2 * 2 + par, par)
                    split_wqk(b + 1, 0)
                else:
                    with act.Fori(0, NCH // 2 - 1) as c2:
                        for par in range(2):
                            chunk_step(b, c2 * 2 + par, par)
                chunk_step(b, NCH - 2, 0, more=False)
                chunk_step(b, NCH - 1, 1, more=False)
                if more:
                    rows_high(b + 1)

            act.wait_ge(wqk_ok, 1)
            split_wqk(0, 0)
            for j in range(TT):
                norm_rows(0, j)
            rows_high(0)
            act.wait_ge(bst_ok, 2)
            with act.Fori(0, NB - 1) as b:
                batch(b, True)
            batch(NB - 1, False)

        @block.vector
        def _(dve):
            v = nc.vector
            own = [0]

            def step(ins):
                own[0] += 1
                return ins.then_inc(dve_own, 1)

            def settle():
                dve.wait_ge(dve_own, own[0])

            def link(ins):
                step(ins)
                settle()

            step(v.memset(ge[:, 0, :], 1.0))
            step(v.memset(ge[:, E, :], 0.0))
            step(v.memset(small[:, :, :], 0.0))
            dve.wait_ge(ids_in, 16)
            link(v.tensor_copy(idf[:, :], idst[:, :]))
            for e in range(1, E):
                step(v.tensor_scalar(ge[:, e, :], idf[:, :], float(e * PER_EXPERT), None, ALU.is_ge))
            settle()
            v.tensor_tensor(oh[:, :, :], ge[:, 0:E, :], ge[:, 1:E + 1, :], ALU.subtract).then_inc(onehot_ok, 1)
            dve.wait_ge(ranks_ok, 1)
            dve.wait_ge(onehot_ok, 1)
            link(v.tensor_copy(cnt[:, :, :].rearrange("p a b -> p (a b)"), bank[0][:, 0:2 * E * NT]))
            total = cnt[:, 1, :]
            dve.wait_ge(const_ok, 6)
            link(v.tensor_tensor_scan(cum[:, :], ones[:, 0:E * NT], total, 0.0, ALU.mult, ALU.add))
            link(v.tensor_tensor(exc[:, :], cum[:, :], total, ALU.subtract))
            pef = pe_[:, :, :].rearrange("p e t -> p (e t)")
            link(v.tensor_tensor(pef, exc[:, :], cnt[:, 0, :], ALU.add))
            link(v.tensor_tensor(pef, pef, oh[:, :, :].rearrange("p e t -> p (e t)"), ALU.mult))
            link(v.tensor_reduce(posf[:, :], pe_[:, :, :].rearrange("p e t -> p t e"), AXX, ALU.add))
            v.tensor_copy(pos[:, :], posf[:, :]).then_inc(pos_ok, 1)
            def slot(k, width=8, start=0):
                return nr[:, 8 * k + start:8 * k + start + width]

            def aggregate(n, mark, done):
                done()
                mark(v.memset(slot(CARRIER), 0.0))
                for j in range(n):
                    mark(v.bn_aggr(mv[:, j, :], st[:, 6 * j:6 * j + 6]))
                done()

            def root_guess(mark, done):
                mark(v.tensor_scalar(nri[:, :], slot(ARG).bitcast(I32), 1, None, ALU.arith_shift_right))
                done()
                mark(v.tensor_scalar(slot(ROOT).bitcast(I32), nri[:, :], -1.0, float(0x5F3759DF), ALU.mult, ALU.add))
                done()

            def root_step(mark, done):
                mark(v.tensor_tensor(slot(TA), slot(ROOT), slot(ROOT), ALU.mult))
                done()
                mark(v.tensor_tensor(slot(TB), slot(TA), slot(ARG), ALU.mult))
                done()
                mark(v.tensor_scalar(slot(TA), slot(TB), -0.5, 1.5, ALU.mult, ALU.add))
                done()
                mark(v.tensor_tensor(slot(ROOT), slot(ROOT), slot(TA), ALU.mult))
                done()

            ARG, ROOT, TA, TB, SM, T1, T2, CARRIER = range(8)
            for half in range(2):
                for j in range(8):
                    if j % 4 == 0:
                        dve.wait_ge(x_in[2 * half + j // 4], 16)
                    step(v.bn_stats(st[:, 6 * j:6 * j + 6], big[:, 8 * half + j, :]))
                aggregate(8, step, settle)
                link(v.tensor_scalar(slot(ARG), mv[:, :, 1], LN_EPS, None, ALU.add))
                root_guess(step, settle)
                for _ in range(3):
                    root_step(step, settle)
                link(v.scalar_tensor_tensor(out=lnb[:, 8 * half:8 * half + 8], in0=mv[:, :, 0], scalar=-1.0,
                                            in1=slot(ROOT), op0=ALU.mult, op1=ALU.mult))
                v.tensor_copy(lna[:, 8 * half:8 * half + 8], slot(ROOT)).then_inc(norm_ok, 1)

            def expert_low(e):
                dve.wait_ge(exp_hi, e + 1)
                v.tensor_tensor(wr[:, LO, e * EW:(e + 1) * EW], stream[:, e % 2, :],
                                wr[:, HI, e * EW:(e + 1) * EW].bitcast(F32), ALU.subtract).then_inc(exp_lo, 1)

            expert_low(0)
            expert_low(1)
            OFF, CNT, NTF, TIN, TEX, DD, DIF = range(7)
            off, excv, cumv = small[:, OFF, :], exc[:, :].rearrange("p (e t) -> p e t", e=E), cum[:, :].rearrange("p (e t) -> p e t", e=E)
            link(v.tensor_copy(off, excv[:, :, 0]))
            link(v.tensor_tensor(small[:, CNT, :], cumv[:, :, NT - 1], off, ALU.subtract))
            link(v.tensor_scalar(nti[:, :], small[:, CNT, :], float(P - 1), None, ALU.add))
            link(v.tensor_scalar(nti[:, :], nti[:, :], P.bit_length() - 1, None, ALU.logical_shift_right))
            link(v.tensor_copy(small[:, NTF, :], nti[:, :]))
            link(v.tensor_tensor_scan(small[:, TIN, :], ones[:, 0:E], small[:, NTF, :], 0.0, ALU.mult, ALU.add))
            link(v.tensor_tensor(small[:, TEX, :], small[:, TIN, :], small[:, NTF, :], ALU.subtract))
            link(v.scalar_tensor_tensor(out=small[:, DD, :], in0=small[:, TEX, :], scalar=-float(P), in1=off,
                                        op0=ALU.mult, op1=ALU.add))
            link(v.tensor_tensor(small[:, DIF, 1:E], small[:, DD, 1:E], small[:, DD, 0:E - 1], ALU.subtract))
            step(v.tensor_scalar(its[:, 0, :], itf[:, :], float(P), None, ALU.mult))
            step(v.memset(its[:, 1, :], 0.0))
            settle()
            for e in range(1, E):
                edge = small[:, TEX, e:e + 1]
                step(v.tensor_scalar(its[:, 2, :], itf[:, :], edge, small[:, DIF, e:e + 1], ALU.is_ge, ALU.mult))
                link(v.scalar_tensor_tensor(out=its[:, 1, :], in0=itf[:, :], scalar=edge, in1=its[:, 1, :],
                                            op0=ALU.is_ge, op1=ALU.add))
                link(v.tensor_tensor(its[:, 0, :], its[:, 0, :], its[:, 2, :], ALU.add))
            step(v.tensor_scalar(itab[:, 0, :], its[:, 0, :], float(T), None, ALU.min))
            step(v.tensor_scalar(itab[:, 1, :], its[:, 1, :], float(EW), None, ALU.mult))
            dve.wait_ge(dve_own, own[0])
            v.tensor_copy(small[:, 15, :], small[:, DD, :]).then_inc(items_ok, 1)

            expert_low(2)
            expert_low(3)
            def x_low(i):
                dve.wait_ge(xt_hi, i + 1)
                v.tensor_tensor(xTs[:, LO, :], bank[4][:, :], xTs[:, HI, :].bitcast(F32),
                                ALU.subtract).then_inc(xt_lo, 1)

            def gated(i):
                dve.wait_ge(h_silu, i + 1)
                v.tensor_tensor(act_sb[:, :], bank[5][:, :], sil[:, :], ALU.mult).then_inc(h_gated, 1)

            def act_low(i):
                dve.wait_ge(at_hi, i + 1)
                v.tensor_tensor(aTs[:, LO, :], bank[6][:, :], aTs[:, HI, :].bitcast(F32),
                                ALU.subtract).then_inc(at_lo, 1)

            x_low(0)
            gated(0)
            x_low(1)
            act_low(0)
            with dve.Fori(1, ITEMS - 1) as i:
                gated(i)
                x_low(i + 1)
                act_low(i)
            gated(ITEMS - 1)
            act_low(ITEMS - 1)

            dve.wait_ge(wqk_in, 16 * LOADS)
            for dt in range(DT):
                v.tensor_scalar(wqk_v[:, 0, dt, :], wqk_v[:, 0, dt, :], lns[:, 0, dt:dt + 1], SCALE, ALU.mult, ALU.mult)
                ins = v.tensor_scalar(wqk_v[:, 1, dt, :], wqk_v[:, 1, dt, :], lns[:, 0, dt:dt + 1], None, ALU.mult)
            ins.then_inc(wqk_ok, 1)
            dve.wait_ge(y_done, ITEMS)
            v.memset(vst.bitcast(F32), 0.0).then_inc(vst_zero, 1)
            v.memset(zst[:, :].bitcast(F32), 0.0).then_inc(vst_zero, 1)
            v.memset(slot(CARRIER), 0.0).then_inc(fin_out, 1)
            link(v.memset(bd[:, :, :, :], 0.0))
            dve.wait_ge(woa_ok, 1)
            woa = bank[1][:, 0:DT * R].rearrange("p (c r) -> p c r", c=DT)
            for h in range(QH):
                rows = slice(HD * h, HD * h + HD)
                ins = v.tensor_copy(bd[rows, :, h, :], woa[rows, :, :])
            ins.then_inc(bd_ok, 1)

            def low(dst, src, high, done):
                v.tensor_tensor(dst, src, high.bitcast(F32), ALU.subtract).then_inc(done, 1)

            def qk_low(b, q, which, at=QKB):
                dve.wait_ge(qk_hi, (b * NQ + q) * 2 + which + 1)
                low(qk[:, (Q_LO, K_LO)[which], :], bank[at][:, :], qk[:, (Q_HI, K_HI)[which], :], qk_lo)

            def maxima(n):
                for i, qts in enumerate(((3,), (2, 0), (1,))):
                    dve.wait_ge(s_done, n * 3 + i + 1)
                    for qt in qts:
                        bk, col, _ = SCORE[qt]
                        v.reduce_max(nb[:, qt:qt + 1], bank[bk][:, col:col + P * (qt + 1)], AXX,
                                     negate=True).then_inc(nb_ok, 1)

            def normalise(n, par):
                dve.wait_ge(exp_ok, n * 4 + 4)
                v.reciprocal(rr[:, par, :], rs[:, par, :]).then_inc(rr_ok, 1)
                dve.wait_ge(rr_ok, n + 1)
                for qt in NORM_DVE:
                    rows = prob_rows(par, qt)
                    v.tensor_scalar(rows, rows, rr[:, par, qt:qt + 1], None, ALU.mult).then_inc(pn_ok, 1)

            def head_step(b, q, j, ahead):
                one_more, two_more = ahead or j < QH - 1, ahead or j < QH - 2
                n = (b * NQ + q) * QH + j
                if one_more:
                    normalise(n + 1, (j + 1) % 2)
                if j < 2 and ahead:
                    qk_low(b, q + 1, j)
                if two_more:
                    maxima(n + 2)
                for i, (bk, w, at) in enumerate(((4, 512, 0), (5, 512, 512), (6, 256, 1024))):
                    dve.wait_ge(pt_hi, n * 3 + i + 1)
                    low(pts[:, j % 2, LO, at:at + w], bank[bk][:, 0:w], pts[:, j % 2, HI, at:at + w], pt_lo)
                if j == 0:
                    dve.wait_ge(vst_hi, b * NQ + q + 1)
                    low(vst_v[:, :, :, 32:32 + R], vp[:, :, bass.ds(q * QH, QH), :], vst_v[:, :, :, 0:R], vst_lo)

            def quad(b, q, ahead):
                for j in range(QH):
                    head_step(b, q, j, ahead)

            def gate_up_low(b, c, par):
                dve.wait_ge(cg_hi, b * NCH + c + 1)
                raw, high, dst = (gu_view(t) for t in (stream[:, par, 0:CW], wch[:, par, HI, 0:CW], wch[:, par, LO, 0:CW]))
                for dt in range(DT):
                    ins = v.scalar_tensor_tensor(out=dst[:, :, dt, :], in0=raw[:, :, dt, :], scalar=lns[:, 1, dt:dt + 1],
                                                 in1=high[:, :, dt, :].bitcast(F32), op0=ALU.mult, op1=ALU.subtract)
                v.tensor_copy(bchunk[:, par, :], bst[:, bass.ds(c * P, P)].bitcast(F32)).then_inc(cg_lo, 1)

            def down_low(b, c, par):
                dve.wait_ge(cd_hi, b * NCH + c + 1)
                low(wch[:, par, LO, CW:CW + D], stream[:, par, CW:CW + D], wch[:, par, HI, CW:CW + D], cd_lo)

            def chunk_step(b, c, par, more=True):
                n = b * NCH + c
                down_low(b, c, par)
                dve.wait_ge(g_silu, n + 1)
                dve.wait_ge(u_done, n + 1)
                v.tensor_tensor(act_sb[:, :], bank[UP][:, :], sil[:, :], ALU.mult).then_inc(gu_ok, 1)
                dve.wait_ge(gu_hi, n + 1)
                low(actr[:, par, LO, :], act_sb[:, :], actr[:, par, HI, :], gu_lo)
                dve.wait_ge(gu_lo, n + 1)
                if more:
                    gate_up_low(b, c + 2, par)

            def x1_tile(b, j):
                dve.wait_ge(x1_in, b * 16 + 16)
                if type(b) is int:
                    dve.wait_ge(y_first[j], 16)
                else:
                    dve.wait_ge(y_in, b * (16 * TT))
                dve.wait_ge(tanh_ok, 1)
                rows = x1f[:, bass.ds(j * D, D)]
                v.scalar_tensor_tensor(out=rows, in0=hbf[:, bass.ds(j * D, D)], scalar=tg[:, 0:1], in1=rows,
                                       op0=ALU.mult, op1=ALU.add).then_inc(ln_own, 1)
                dve.wait_ge(ln_own, b * K_LN + j * 2 + 1)
                v.bn_stats(st[:, bass.ds(j * 6, 6)], rows).then_inc(ln_own, 1)

            def norm_factors(b, half):
                mine = [2 * TT if half == 0 else 2 * TT + 13]

                def mark(ins):
                    mine[0] += 1
                    ins.then_inc(ln_own, 1)

                def done():
                    dve.wait_ge(ln_own, b * K_LN + mine[0])

                mean, var = mv[:, 0:TT, 0], mv[:, 0:TT, 1]
                r1, r2 = slot(ROOT, TT), slot(ROOT, TT, TT)
                if half == 0:
                    aggregate(TT, mark, done)
                    mark(v.tensor_scalar(slot(ARG, TT), var, LN_EPS, None, ALU.add))
                    done()
                    mark(v.scalar_tensor_tensor(out=slot(ARG, TT, TT), in0=slot(ARG, TT), scalar=RMS_EPS, in1=var,
                                                op0=ALU.mult, op1=ALU.add))
                    done()
                    root_guess(mark, done)
                    root_step(mark, done)
                    assert mine[0] == 2 * TT + 13, mine[0]
                    return
                for _ in range(2):
                    root_step(mark, done)
                mark(v.scalar_tensor_tensor(out=lnb[:, 0:TT], in0=mean, scalar=-1.0, in1=r2,
                                            op0=ALU.mult, op1=ALU.mult))
                mark(v.tensor_scalar(slot(T1, TT), r1, tg[:, 1:2], None, ALU.mult))
                done()
                mark(v.scalar_tensor_tensor(out=slot(T2, TT), in0=mean, scalar=-1.0, in1=slot(T1, TT),
                                            op0=ALU.mult, op1=ALU.mult))
                mark(v.tensor_scalar(slot(SM, TT), slot(T1, TT), 1.0, None, ALU.add))
                done()
                v.tensor_copy(lna[:, 0:TT], r2).then_inc(ln_ok, 1)
                assert mine[0] == K_LN - TT, mine[0]

            def residual(b, j):
                rows = x1f[:, bass.ds(j * D, D)]
                factor, term = nr[:, bass.ds(j + 8 * SM, 1)], nr[:, bass.ds(j + 8 * T2, 1)]
                dve.wait_ge(hb_ok, b * TT + j + 1)
                v.tensor_scalar(rows, rows, factor, term, ALU.mult, ALU.add).then_inc(ln_own, 1)

            def rows_low(b):
                for dt in range(DT):
                    dve.wait_ge(ht_hi, b * 4 + dt + 1)
                    low(hT[:, LO, dt, :], bank[ROWS[dt]][:, :], hT[:, HI, dt, :], ht_lo)

            def batch(b, more):
                for which in range(2):
                    qk_low(b, 0, which, FIRST_QK[which])
                dve.wait_ge(ha_low, b + 1)
                v.tensor_tensor(haT, bank[LOW_RANK][0:R, :], att_low, ALU.add).then_inc(ha_ok, 1)
                maxima(b * H)
                normalise(b * H, 0)
                maxima(b * H + 1)
                with dve.Fori(0, NQ - 2) as q:
                    quad(b, q, 2)
                quad(b, NQ - 2, 1)
                quad(b, NQ - 1, 0)
                gate_up_low(b, 0, 0)
                dve.wait_ge(at_low, b + 1)
                v.tensor_tensor(att_sum, bank[ATT][0:R, :], att_low, ALU.add).then_inc(at_sum, 1)
                gate_up_low(b, 1, 1)
                dve.wait_ge(mod_ok, b + 1)
                v.scalar_tensor_tensor(out=zrow, in0=att_low, scalar=MOD_SCALE, in1=haT,
                                       op0=ALU.mult, op1=ALU.mult).then_inc(z_ok, 1)
                dve.wait_ge(zs_hi, b + 1)
                low(zst[32:32 + R, :], zrow, zst[0:R, :], zs_ok)
                if more:
                    for par in range(2):
                        chunk_step(b, par, par)
                    with dve.Fori(1, 1 + TT // 2) as c2:
                        for par in range(2):
                            chunk_step(b, c2 * 2 + par, par)
                            x1_tile(b + 1, c2 * 2 + par - 2)
                    for par in range(2):
                        chunk_step(b, 2 + TT + par, par)
                        norm_factors(b + 1, par)
                    with dve.Fori(NORM_AT, NORM_AT + TT // 2) as c2:
                        for par in range(2):
                            chunk_step(b, c2 * 2 + par, par)
                            residual(b + 1, c2 * 2 + par - 2 * NORM_AT)
                    with dve.Fori(NORM_AT + TT // 2, NCH // 2 - 1) as c2:
                        for par in range(2):
                            chunk_step(b, c2 * 2 + par, par)
                else:
                    with dve.Fori(0, NCH // 2 - 1) as c2:
                        for par in range(2):
                            chunk_step(b, c2 * 2 + par, par)
                chunk_step(b, NCH - 2, 0, more=False)
                chunk_step(b, NCH - 1, 1, more=False)
                if more:
                    rows_low(b + 1)
                dve.wait_ge(res_in, b * 16 + 16)
                if more:
                    dve.wait_ge(d_done, (b + 1) * NCH)
                for tt in range(TT):
                    if not more:
                        dve.wait_ge(d_done, (b + 1) * NCH + tt)
                    ins = v.scalar_tensor_tensor(out=xt[:, tt, :], in0=bank[Y0 + tt][:, :], scalar=tg[:, 1:2],
                                                 in1=xt[:, tt, :], op0=ALU.mult, op1=ALU.add)
                    if tt == TT - 1 or not more:
                        ins.then_inc(fin_out, 1)

            for j in range(TT):
                x1_tile(0, j)
            norm_factors(0, 0)
            norm_factors(0, 1)
            dve.wait_ge(vw_hi, DT)
            for dt in range(DT):
                ins = v.scalar_tensor_tensor(
                    out=vw[:, LO, dt, :], in0=bank[2 + dt // 2][:, 256 * (dt % 2):256 * (dt % 2) + 256],
                    scalar=lns[:, 0, dt:dt + 1], in1=vw[:, HI, dt, :].bitcast(F32), op0=ALU.mult, op1=ALU.subtract)
            ins.then_inc(prep_ok, 1)

            for j in range(TT):
                residual(0, j)
            rows_low(0)
            with dve.Fori(0, NB - 1) as b:
                batch(b, True)
            batch(NB - 1, False)


def kernel(x, itok_BxS_13_99985, ctx_2048, g_xattn, g_ffn, L0_ffn_ln1_w, L0_ffn_ln2_w, L0_ffn_Wq, L0_ffn_Wk,
           L0_ffn_Wv, L0_ffn_Wo, L0_ffn_A, L0_ffn_B, L0_ffn_W_in_base, L0_ffn_W_up_base, L0_ffn_W_down):
    import concourse.bacc as bacc
    import numpy as np
    from concourse.bass_utils import run_bass_kernel_spmd

    def c(a):
        return np.ascontiguousarray(a)

    def by_row(w):
        w = np.asarray(w)
        return w.reshape(-1, P, w.shape[-1]).transpose(1, 0, 2).reshape(P, -1)

    ctx_2048 = np.asarray(ctx_2048)
    wi, wu = (np.asarray(w).reshape(NCH, P, DT, P).transpose(3, 0, 2, 1).reshape(P, NCH, DT * P)
              for w in (L0_ffn_W_in_base, L0_ffn_W_up_base))
    wd = np.asarray(L0_ffn_W_down).T.reshape(NCH, P, D).transpose(1, 0, 2)
    arrays = {
        "x": c(np.asarray(x).reshape(T, D)),
        "ids": c(np.asarray(itok_BxS_13_99985).reshape(NT, P).T),
        "wexp": c(np.stack([by_row(ctx_2048[e].T) for e in range(E)], 1)),
        "wov": c(np.stack([by_row(L0_ffn_Wo), by_row(L0_ffn_Wv)], 1)),
        "amat": c(by_row(L0_ffn_A).reshape(P, DT, R)),
        "bmat": c(np.asarray(L0_ffn_B)),
        "ln": c(np.stack([np.asarray(w).reshape(DT, P).T for w in (L0_ffn_ln1_w, L0_ffn_ln2_w)], 1)),
        "gates": c(np.stack([np.asarray(g_xattn), np.asarray(g_ffn)], 1)),
        "wqk": c(np.stack([by_row(np.asarray(w).T) for w in (L0_ffn_Wq, L0_ffn_Wk)], 1)),
        "wmlp": c(np.concatenate([wi, wu, wd], 2)),
    }
    nc = bacc.Bacc("TRN2", target_bir_lowering=False, num_devices=1)
    args = {n: nc.dram_tensor(f"in_{n}", a.shape, mybir.dt.from_np(a.dtype), kind="ExternalInput").ap()
            for n, a in arrays.items()}
    out = nc.dram_tensor("out", [T, D], F32, kind="ExternalOutput").ap()
    build(nc, **args, out=out)
    got = run_bass_kernel_spmd(nc, [{f"in_{n}": a for n, a in arrays.items()}], core_ids=[0]).results[0]["out"]
    return got.reshape(NB, S, D)
```
